# Optimizing a Trainium2 kernel written in Bass

```python
import numpy as np
import jax
import jax.numpy as jnp

def _softmax(x, axis=-1):
    return jax.nn.softmax(x, axis=axis)

def _gelu(x):
    return jax.nn.gelu(x, approximate=True)

def _silu(x):
    return jax.nn.silu(x)

def _sigmoid(x):
    return jax.nn.sigmoid(x)

def _layernorm(x, axis=-1, eps=1e-05):
    m = jnp.mean(x, axis=axis, keepdims=True)
    v = jnp.var(x, axis=axis, keepdims=True)
    return (x - m) / jnp.sqrt(v + eps)

def _scatter_add(tgt, idx, src, axis=0):
    return tgt.at[idx].add(src)

def _segment_sum(src, seg, n):
    return jax.ops.segment_sum(src, seg, n)
kernel_name = 'mk_gnn_preln_d2_gnn_r64_fc0254'

def setup_inputs(seed: int=0):
    np.random.seed(seed)
    _w = jnp.asarray

    def _rec_inputs():
        import jax
        import jax.numpy as jnp
        _gk = jax.random.key(seed)
        x = -0.0005121 + 1.001 * jax.random.normal(jax.random.fold_in(_gk, 1), (100000, 64), jnp.float32)
        src = jax.random.randint(jax.random.fold_in(_gk, 2), (50000,), 0, 100000, jnp.int32)
        dst = jnp.minimum((100000 * jax.random.uniform(jax.random.fold_in(_gk, 3), (50000,)) ** 2.0).astype(jnp.int32), 99999)
        _o = jnp.argsort(dst, stable=True)
        src = src[_o]
        dst = dst[_o]
        return (x, src, dst)
    x, src, dst = _rec_inputs()

    def _L0_gnn_setup():
        import jax, jax.numpy as jnp
        import numpy as np
        N, E, C, H = (50000, 12500, 64, 64)
        EPS = 1e-05

        def _edge_conv(x, src, dst, Wa, ba, Wb, bb):
            xi = x[dst]
            xj = x[src]
            h = jnp.concatenate([xi, xj - xi], axis=-1)
            h = jax.nn.relu(h @ Wa + ba)
            h = jax.nn.relu(h @ Wb + bb)
            out = jax.ops.segment_max(h, dst, num_segments=x.shape[0])
            return jnp.where(jnp.isneginf(out), 0.0, out)

        def _batchnorm(x, gamma, beta):
            mean = jnp.mean(x, axis=0)
            var = jnp.var(x, axis=0)
            return gamma * (x - mean) * jax.lax.rsqrt(var + EPS) + beta
        key = jax.random.key(seed)
        ks = jax.random.split(key, 12)
        x = jax.random.normal(ks[0], (N, C), dtype=jnp.float32)
        edge_index = jax.random.randint(ks[1], (2, E), 0, N, dtype=jnp.int64)
        batch = jnp.zeros((N,), dtype=jnp.int64)
        s1 = 1.0 / np.sqrt(2 * C)
        s2 = 1.0 / np.sqrt(H)
        return {'x': x, 'edge_index': edge_index, 'batch': batch, 'W1a': jax.random.normal(ks[2], (2 * C, H), jnp.float32) * s1, 'b1a': jnp.zeros((H,), jnp.float32), 'W1b': jax.random.normal(ks[3], (H, H), jnp.float32) * s2, 'b1b': jnp.zeros((H,), jnp.float32), 'gamma1': jnp.ones((H,), jnp.float32), 'beta1': jnp.zeros((H,), jnp.float32), 'W2a': jax.random.normal(ks[4], (2 * H, H), jnp.float32) * s2, 'b2a': jnp.zeros((H,), jnp.float32), 'W2b': jax.random.normal(ks[5], (H, H), jnp.float32) * s2, 'b2b': jnp.zeros((H,), jnp.float32), 'gamma2': jnp.ones((H,), jnp.float32), 'beta2': jnp.zeros((H,), jnp.float32)}
    _L0_gnn_all = _L0_gnn_setup()
    _L0_gnn_in = {k: v for k, v in _L0_gnn_all.items() if k in ('W1a', 'b1a', 'W1b', 'b1b', 'gamma1', 'beta1', 'W2a', 'b2a', 'W2b', 'b2b', 'gamma2', 'beta2')}
    del _L0_gnn_all

    def _L1_gnn_setup():
        import jax, jax.numpy as jnp
        import numpy as np

        def gcn_conv(x, src, dst, deg_inv_sqrt, W, b):
            h = x @ W
            norm = deg_inv_sqrt[src] * deg_inv_sqrt[dst]
            msg = h[src] * norm[:, None]
            out = jax.ops.segment_sum(msg, dst, num_segments=x.shape[0])
            return out + b
        key = jax.random.key(seed)
        k_x, k_e, k_w1, k_w2 = jax.random.split(key, 4)
        N, E = (50000, 12500)
        in_dim, hidden_dim, out_dim = (64, 128, 64)
        x = jax.random.normal(k_x, (N, in_dim), dtype=jnp.float32)
        edge_index = jax.random.randint(k_e, (2, E), 0, N, dtype=jnp.int32)
        W1 = jax.random.normal(k_w1, (in_dim, hidden_dim), dtype=jnp.float32) * (1.0 / np.sqrt(in_dim))
        b1 = jnp.zeros((hidden_dim,), dtype=jnp.float32)
        W2 = jax.random.normal(k_w2, (hidden_dim, out_dim), dtype=jnp.float32) * (1.0 / np.sqrt(hidden_dim))
        b2 = jnp.zeros((out_dim,), dtype=jnp.float32)
        return {'x': x, 'edge_index': edge_index, 'W1': W1, 'b1': b1, 'W2': W2, 'b2': b2}
    _L1_gnn_all = _L1_gnn_setup()
    _L1_gnn_in = {k: v for k, v in _L1_gnn_all.items() if k in ('W1', 'b1', 'W2', 'b2')}
    del _L1_gnn_all
    return {'x': x, 'src': src, 'dst': dst, 'L0_gnn_W1a': _L0_gnn_in['W1a'], 'L0_gnn_b1a': _L0_gnn_in['b1a'], 'L0_gnn_W1b': _L0_gnn_in['W1b'], 'L0_gnn_b1b': _L0_gnn_in['b1b'], 'L0_gnn_gamma1': _L0_gnn_in['gamma1'], 'L0_gnn_beta1': _L0_gnn_in['beta1'], 'L0_gnn_W2a': _L0_gnn_in['W2a'], 'L0_gnn_b2a': _L0_gnn_in['b2a'], 'L0_gnn_W2b': _L0_gnn_in['W2b'], 'L0_gnn_b2b': _L0_gnn_in['b2b'], 'L0_gnn_gamma2': _L0_gnn_in['gamma2'], 'L0_gnn_beta2': _L0_gnn_in['beta2'], 'L1_gnn_W1': _L1_gnn_in['W1'], 'L1_gnn_b1': _L1_gnn_in['b1'], 'L1_gnn_W2': _L1_gnn_in['W2'], 'L1_gnn_b2': _L1_gnn_in['b2']}

def reference(x, src, dst, L0_gnn_W1a, L0_gnn_b1a, L0_gnn_W1b, L0_gnn_b1b, L0_gnn_gamma1, L0_gnn_beta1, L0_gnn_W2a, L0_gnn_b2a, L0_gnn_W2b, L0_gnn_b2b, L0_gnn_gamma2, L0_gnn_beta2, L1_gnn_W1, L1_gnn_b1, L1_gnn_W2, L1_gnn_b2):
    import jax
    import jax.numpy as jnp

    def _L0_gnn_ref(x, edge_index, batch, W1a, b1a, W1b, b1b, gamma1, beta1, W2a, b2a, W2b, b2b, gamma2, beta2):
        import jax, jax.numpy as jnp
        import numpy as np
        N, E, C, H = (50000, 12500, 64, 64)
        EPS = 1e-05

        def _edge_conv(x, src, dst, Wa, ba, Wb, bb):
            xi = x[dst]
            xj = x[src]
            h = jnp.concatenate([xi, xj - xi], axis=-1)
            h = jax.nn.relu(h @ Wa + ba)
            h = jax.nn.relu(h @ Wb + bb)
            out = jax.ops.segment_max(h, dst, num_segments=x.shape[0])
            return jnp.where(jnp.isneginf(out), 0.0, out)

        def _batchnorm(x, gamma, beta):
            mean = jnp.mean(x, axis=0)
            var = jnp.var(x, axis=0)
            return gamma * (x - mean) * jax.lax.rsqrt(var + EPS) + beta
        src, dst = (edge_index[0], edge_index[1])
        h = _edge_conv(x, src, dst, W1a, b1a, W1b, b1b)
        h = _batchnorm(h, gamma1, beta1)
        h = _edge_conv(h, src, dst, W2a, b2a, W2b, b2b)
        h = _batchnorm(h, gamma2, beta2)
        return h

    def _L1_gnn_ref(x, edge_index, W1, b1, W2, b2):
        import jax, jax.numpy as jnp
        import numpy as np

        def gcn_conv(x, src, dst, deg_inv_sqrt, W, b):
            h = x @ W
            norm = deg_inv_sqrt[src] * deg_inv_sqrt[dst]
            msg = h[src] * norm[:, None]
            out = jax.ops.segment_sum(msg, dst, num_segments=x.shape[0])
            return out + b
        N = x.shape[0]
        loops = jnp.arange(N, dtype=edge_index.dtype)
        src = jnp.concatenate([edge_index[0], loops])
        dst = jnp.concatenate([edge_index[1], loops])
        deg = jax.ops.segment_sum(jnp.ones_like(dst, dtype=x.dtype), dst, num_segments=N)
        deg_inv_sqrt = jnp.where(deg > 0, jax.lax.rsqrt(jnp.maximum(deg, 1.0)), 0.0)
        h = jax.nn.relu(gcn_conv(x, src, dst, deg_inv_sqrt, W1, b1))
        out = jax.nn.relu(gcn_conv(h, src, dst, deg_inv_sqrt, W2, b2))
        return out
    edge_index = jnp.stack([src, dst])
    batch0 = jnp.zeros((100000,), jnp.int32)
    h = jnp.maximum(_layernorm(x, axis=-1), 0.0)
    x = x + _L0_gnn_ref(h, edge_index, batch0, L0_gnn_W1a, L0_gnn_b1a, L0_gnn_W1b, L0_gnn_b1b, L0_gnn_gamma1, L0_gnn_beta1, L0_gnn_W2a, L0_gnn_b2a, L0_gnn_W2b, L0_gnn_b2b, L0_gnn_gamma2, L0_gnn_beta2)
    h = jnp.maximum(_layernorm(x, axis=-1), 0.0)
    x = x + _L1_gnn_ref(h, edge_index, L1_gnn_W1, L1_gnn_b1, L1_gnn_W2, L1_gnn_b2)
    return x

_drawn_inputs = setup_inputs


def setup_inputs(seed=0):
    import zlib

    import numpy as np

    out = dict(_drawn_inputs(seed))
    spreads = {'L0_gnn_b1a': (0.0, 0.1),
     'L0_gnn_b1b': (0.0, 0.1),
     'L0_gnn_gamma1': (1.0, 0.2),
     'L0_gnn_beta1': (0.0, 0.268),
     'L0_gnn_b2a': (0.0, 0.1),
     'L0_gnn_b2b': (0.0, 0.1),
     'L0_gnn_gamma2': (1.0, 0.2),
     'L0_gnn_beta2': (0.0, 0.1),
     'L1_gnn_b1': (0.0, 0.1),
     'L1_gnn_b2': (0.0, 0.1)}
    factors = {}
    for name, (base, spread) in spreads.items():
        noise = np.random.default_rng([zlib.crc32(name.encode()), seed]).standard_normal(out[name].shape)
        drawn = base * np.exp(spread * noise) if base else spread * noise
        out[name] = jnp.asarray(drawn.astype(out[name].dtype))
    for name, factor in factors.items():
        out[name] = (out[name] * factor).astype(out[name].dtype)
    return out
```

```python
import concourse.bass as bass
import concourse.mybir as mybir
from concourse.alu_op_type import AluOpType as ALU
from contextlib import ExitStack


F32, BF16, I32 = mybir.dt.float32, mybir.dt.bfloat16, mybir.dt.int32
ACT = mybir.ActivationFunctionType
AX = mybir.AxisListType.X

P = 128
N, E, C, HID = 100000, 50000, 64, 128
K = 4
GE = K * P
TILES = -(-E // P)
NG = -(-TILES // (2 * K)) * 2
CH = 4
R = 8
GN = R * P
ND = -(-N // (2 * GN)) * 2
NP = ND * GN
LASTP = (N - (ND - 1) * GN) // R
CB = C + 1
PAD = float(2 ** 20)
EPS = 1e-5
ZA, ZB = 28, 28
ZC = NP * CB // P // ZB
assert (ND - 1) * GN < N and LASTP * R == N - (ND - 1) * GN and NG == ND
assert NP * C // P % ZA == 0 and NP * CB // P % ZB == 0 and NP * C // P // ZA <= ZC
assert CH * P >= NG * K and PAD > N

EC1, EC2, GCN1, GCN2 = range(4)


def build(nc, x, src, dst, W1a, b1a, W1b, b1b, gamma1, beta1, W2a, b2a, W2b, b2b, gamma2, beta2,
          gW1, gb1, gW2, gb2, out):
    def dram(name, shape):
        return nc.dram_tensor(name, shape, F32, kind="Internal").ap()

    tabA = dram("tabA", (NP, C))
    tabB = dram("tabB", (NP, CB))
    m1e = dram("m1e", (NG * P, K * C))
    x1 = dram("x1", (NP, C))
    hs = dram("hs", (NP, C))
    gt = dram("gt", (NP, C))

    def nodes(t, c=C):
        return t.rearrange("(g p r) c -> g p (r c)", p=P, r=R)

    m1e_g = m1e.rearrange("(g p) f -> g p f", p=P)
    tabA_g, tabB_g, x1_g, hs_g, gt_g = (nodes(t) for t in (tabA, tabB, x1, hs, gt))
    FULL = (ND - 1) * GN
    x_g, out_g = nodes(x[0:FULL, :]), nodes(out[0:FULL, :])
    x_last = x[FULL:N, :].rearrange("(p r) c -> p (r c)", r=R)
    out_last = out[FULL:N, :].rearrange("(p r) c -> p (r c)", r=R)

    with ExitStack() as ctx:
        def sb(name, shape, dt=F32):
            return ctx.enter_context(nc.sbuf_tensor(name, shape, dt))

        def sem(name):
            return ctx.enter_context(nc.semaphore(name))

        def two(name, shape, dt=F32):
            return [sb(f"{name}{s}", shape, dt) for s in range(2)]

        zeros = sb("zeros", [P, ZC])
        ident = sb("ident", [P, P])
        rev = sb("rev", [P, P])
        ident16, rev16 = sb("ident16", [P, P], BF16), sb("rev16", [P, P], BF16)
        ones = sb("ones", [P, GE])
        eps = sb("eps", [P, 1])
        raw = sb("raw", [P, 4, CH, P], I32)
        rows = sb("rows", [P, 10, CH, P])
        revrows = sb("revrows", [P, 2, CH * P])
        gidx = sb("gidx", [P, NG, 2 * K], I32)
        sidx = sb("sidx", [P, NG, 2 * K], I32)
        flags = sb("flags", [P, NG, 2 * K], BF16)
        masks = sb("masks", [P, NG, 2 * K])
        Wc = [sb(f"Wc{l}", [P, C]) for l in range(2)]
        Wtmp = sb("Wtmp", [P, 2, C])
        Weff = sb("Weff", [P, C])
        Wb = [sb(f"Wb{l}", [C, C]) for l in range(2)]
        cols = sb("cols", [P, 12])
        B1A, B1B, GA1, BE1, B2A, B2B, GA2, BE2, GB1 = range(9)
        gw1 = sb("gw1", [P, HID])
        gw2 = sb("gw2", [HID, C])
        gb2r = sb("gb2r", [P, C])
        acc = sb("acc", [C, 2])
        bn = sb("bn", [P, 8])
        a1, c1, bias2 = sb("a1", [P, 1]), sb("c1", [P, 1]), sb("bias2", [C, 1])
        diag = sb("diag", [C, 2, C])
        bnrow = sb("bnrow", [P, 2, C])
        gi, si = two("gi", [P, 2 * K], I32), two("si", [P, K], I32)
        fl, mk = two("fl", [P, K], BF16), two("mk", [P, K])
        G = two("G", [P, K, 2 * C])
        xc, sq = sb("xc", [P, 2 * K, C]), sb("sq", [P, 2 * K, C])
        H = two("H", [P, K, 2 * C])
        ln = sb("ln", [P, 5, R])
        TS = two("TS", [P, GE])
        A1 = sb("A1", [C, GE])
        A2 = two("A2", [C, GE])
        M = two("M", [CB, GE])
        MT = two("MT", [P, K, CB])
        MQ = two("MQ", [P, K, C])
        dis = sb("dis", [P, ND, R])
        deg = two("deg", [P, R])
        DA, DB, DC = two("DA", [P, R, C]), two("DB", [P, R, CB]), two("DC", [P, R, C])
        U, V = two("U", [P, R, C]), two("V", [P, R, C])
        Z, O = two("Z", [P, R, C]), two("O", [P, R, C])
        HT = sb("HT", [P, 2, GE])

        bank = [ctx.enter_context(nc.psum_tensor(f"bank{b}", [P, GE], F32)) for b in range(8)]
        pT, pU1, pU2, pB, pS = bank[0], bank[3], bank[4], bank[5], [bank[6], bank[7]]
        pF = [bank[1], bank[2]]
        pBk = pB[:, 0:K * CB].rearrange("p (k c) -> p k c", c=CB)
        pH, pG = [bank[3], bank[4]], bank[5]

        s_held = sem("held")
        s_const, s_ident, s_zero = sem("const_built"), sem("ident_ready"), sem("zero_ready")
        s_raw, s_wts, s_pad = sem("raw_loaded"), sem("weights_loaded"), sem("pad_written")
        s_zA, s_zB = sem("tabA_cleared"), sem("tabB_cleared")
        s_rows, s_rowsT, s_revrows, s_revT, s_idx = (sem(n) for n in (
            "rows_ready", "rows_turned", "revrows_ready", "revrows_turned", "indices_ready"))
        s_wcat, s_set = sem("weights_stacked"), sem("setup_step")
        s_gi, s_si = [sem(f"gather_idx{s}") for s in range(2)], [sem(f"scatter_idx{s}") for s in range(2)]
        s_g, s_sc = [sem(f"gathered{s}") for s in range(2)], [sem(f"scattered{s}") for s in range(2)]
        s_ml, s_ms = [sem(f"m1e_loaded{s}") for s in range(2)], [sem(f"m1e_stored{s}") for s in range(2)]
        s_fl, s_mk, s_flT = sem("flags_staged"), sem("masks_staged"), sem("flags_spread")
        s_sum, s_mean, s_xc, s_sq, s_ssq, s_std, s_rstd, s_h = (sem(n) for n in (
            "ln_sum", "ln_mean", "ln_centred", "ln_squared", "ln_sumsq", "ln_std", "ln_rstd", "ln_out"))
        s_T, s_TS, s_back = sem("turned"), sem("turned_copied"), sem("dst_spread")
        s_u1, s_a1, s_u2, s_a2 = sem("layer1_sum"), sem("layer1_out"), sem("layer2_sum"), sem("layer2_out")
        s_scan, s_cnt, s_mT, s_mt, s_mq = (sem(n) for n in (
            "scanned", "counted", "result_turned", "result_copied", "result_squared"))
        s_st, s_acc = sem("stats_sum"), sem("stats_added")
        s_bn, s_bnsd, s_bnp, s_fold = sem("bn_step"), sem("bn_std"), sem("bn_product"), sem("bn_folded")
        s_ld = [[sem(f"dense_loaded{ph}{s}") for s in range(2)] for ph in range(3)]
        s_wr = [[sem(f"dense_stored{ph}{s}") for s in range(2)] for ph in range(3)]
        s_v, s_x1, s_used, s_o = sem("dense_shifted"), sem("stream_ready"), sem("dense_used"), sem("dense_out")
        s_deg, s_dis, s_dsq, s_drs = sem("degree_root"), sem("dis_ready"), sem("dense_squared"), sem("dense_rstd")
        s_z0, s_z, s_zT, s_zTS = sem("agg_added"), sem("agg_scaled"), sem("agg_turned"), sem("agg_copied")
        s_hm, s_hr, s_gm = sem("hidden_sum"), sem("hidden_out"), sem("gcn_product")
        s_f0, s_f1, s_f2 = sem("final_added"), sem("final_scaled"), sem("final_biased")

        def need(eng, s, value):
            if not (isinstance(value, int) and value <= 0):
                eng.wait_ge(s, value)

        def held(eng):
            eng.sem_inc(s_held, 1)

        def run(eng, step, last=None):
            for h in range(2):
                step(h, 0)
                step(h, 1)
            if last is None:
                with eng.Fori(2, NG // 2) as h:
                    step(h, 0)
                    step(h, 1)
            else:
                with eng.Fori(2, NG // 2 - 1) as h:
                    step(h, 0)
                    step(h, 1)
                step(NG // 2 - 1, 0)
                last(NG // 2 - 1, 1)

        def done(ph, h, s):
            return NG * ph + 2 * h + s + 1

        def gath(ph, h):
            before = 0 if ph == EC1 else 16 * K * (NG // 2) * (ph + 1)
            return before + 16 * K * (2 if ph == EC1 else 1) * (h + 1)

        def scat(ph, h):
            return 16 * K * ((NG // 2) * ph + h + 1)

        def group(ph, h, s):
            return (NG - 1 - s) - 2 * h if ph == EC2 else 2 * h + s

        block = ctx.enter_context(nc.Block())

        @block.sync
        def _(sp):
            sp.wait_ge(s_pad, 1)
            W = P * (CH - 1)
            T6 = E // P - W
            rest = E - (E // P) * P

            def load_rows(a, v, shift):
                last = rest - max(shift, 0)
                if shift >= 0:
                    full = v[shift:shift + W * P].rearrange("(c t e) -> t c e", t=P, e=P)
                    sp.dma_start(raw[:, a, 0:CH - 1, :], full).then_inc(s_raw, 16)
                else:
                    sp.dma_start(raw[0:1, a, 0, 1:P], v[0:P - 1].rearrange("(t e) -> t e", t=1)).then_inc(s_raw, 16)
                    sp.dma_start(raw[1:P, a, 0, :], v[P - 1:P - 1 + (P - 1) * P].rearrange("(t e) -> t e", e=P)).then_inc(s_raw, 16)
                    sp.dma_start(raw[:, a, 1:CH - 1, :], v[P * P - 1:W * P - 1].rearrange("(c t e) -> t c e", t=P, e=P)).then_inc(s_raw, 16)
                b = W * P + shift
                sp.dma_start(raw[0:T6, a, CH - 1, :], v[b:b + T6 * P].rearrange("(t e) -> t e", e=P)).then_inc(s_raw, 16)
                b += T6 * P
                sp.dma_start(raw[T6:T6 + 1, a, CH - 1, 0:last], v[b:b + last].rearrange("(t e) -> t e", t=1)).then_inc(s_raw, 16)

            load_rows(0, src, 0)
            load_rows(1, dst, 0)
            load_rows(2, dst, 1)
            load_rows(3, dst, -1)
            for l, (wa, wb) in enumerate(((W1a, W1b), (W2a, W2b))):
                sp.dma_start(Wc[l][0:C, :], wa[C:2 * C, :]).then_inc(s_wts, 16)
                sp.dma_start(Wc[l][C:P, :], wa[0:C, :]).then_inc(s_wts, 16)
                sp.dma_start(Wtmp[C:P, l, :], wa[C:2 * C, :]).then_inc(s_wts, 16)
                sp.dma_start(Wb[l][:, :], wb[:, :]).then_inc(s_wts, 16)
            for j, v in ((B1A, b1a), (B1B, b1b), (GA1, gamma1), (BE1, beta1), (B2A, b2a), (B2B, b2b),
                         (GA2, gamma2), (BE2, beta2), (GB1, gb1)):
                sp.dma_start(cols[0:v.shape[0], j:j + 1], v.rearrange("(p a) -> p a", a=1)).then_inc(s_wts, 16)
            sp.dma_start(gw1[0:C, :], gW1[:, :]).then_inc(s_wts, 16)
            sp.dma_start(gw1[C:P, :], gW1[:, :]).then_inc(s_wts, 16)
            sp.dma_start(gw2[:, :], gW2[:, :]).then_inc(s_wts, 16)
            sp.dma_start(gb2r[:, :], gb2.rearrange("(a c) -> a c", a=1).to_broadcast([P, C])).then_inc(s_wts, 16)
            sp.wait_ge(s_idx, 1)

            def stage(ph, h, s, back):
                need(sp, s_g[s], gath(ph, h - 1) if not (isinstance(h, int) and h == 0 and ph == EC1) else 0)
                held(sp)
                n = 2 * K if ph == EC1 else K
                sp.dma_start(gi[s][:, 0:n], gidx[:, bass.ds(group(ph, h, s), 1), 0:n].rearrange("p a n -> p (a n)")).then_inc(s_gi[s], 16)

            def stage_scatter(ph, h, s):
                need(sp, s_sc[s], scat(ph, h - 1))
                held(sp)
                o = K if ph == EC2 else 0
                sp.dma_start(si[s][:, :], sidx[:, bass.ds(group(ph, h, s), 1), o:o + K].rearrange("p a n -> p (a n)")).then_inc(s_si[s], 16)

            def edge_loads(ph):
                def step(h, s):
                    stage(ph, h, s, 0)
                    if ph == EC2:
                        sp.wait_ge(s_T, done(ph, h, s) - 2)
                        sp.dma_start(G[s][:, :, C:2 * C], m1e_g[bass.ds(group(ph, h, s), 1), :, :].rearrange("a p (k c) -> p (a k) c", c=C)).then_inc(s_ml[s], 16)
                    if not (isinstance(h, int) and h == 0):
                        tail(ph, h - 1, s)

                def tail(ph, h, s):
                    stage_scatter(ph, h, s)
                    if ph == EC1:
                        sp.wait_ge(s_mt, done(ph, h, s))
                        sp.dma_start(m1e_g[bass.ds(group(ph, h, s), 1), :, :].rearrange("a p (k c) -> p (a k) c", c=C), MT[s][:, :, 0:C]).then_inc(s_ms[s], 16)

                run(sp, step)
                tail(ph, NG // 2 - 1, 0)
                tail(ph, NG // 2 - 1, 1)

            edge_loads(EC1)
            for s in range(2):
                sp.wait_ge(s_ms[s], 16 * (NG // 2))
            edge_loads(EC2)
            for s in range(2):
                sp.wait_ge(s_sc[s], scat(EC2, NG // 2 - 1))

            def dense(ph, loads, stores):
                used, base = ((s_dis, 0), (s_used, 0), (s_o, 2 * ND))[ph]

                def store(h, s, last=False):
                    sp.wait_ge(s_o, done(ph, h, s))
                    for d, t in stores(h, s, last):
                        sp.dma_start(d, t).then_inc(s_wr[ph][s], 16)

                def step(h, s, last=False):
                    if not (isinstance(h, int) and h == 0):
                        sp.wait_ge(used, base + 2 * h + s - 1)
                    for t, d in loads(h, s, last):
                        sp.dma_start(t, d).then_inc(s_ld[ph][s], 16)
                    if s == 1:
                        store(h, 0)
                    elif not (isinstance(h, int) and h == 0):
                        store(h - 1, 1)

                run(sp, step, lambda h, s: step(h, s, True))
                store(NG // 2 - 1, 1, True)

            def at(t, h, s):
                return t[bass.ds(2 * h + s, 1), :, :].rearrange("a p f -> p (a f)")

            def flat(t):
                return t[:, :, :].rearrange("p r c -> p (r c)")

            def node_io(h, s, last, tile, whole, part):
                if last:
                    return flat(tile)[0:LASTP, :], part
                return flat(tile), at(whole, h, s)

            dense(0, lambda h, s, last: [node_io(h, s, last, DA[s], x_g, x_last), (flat(DB[s]), at(tabB_g, h, s))],
                  lambda h, s, last: [(at(x1_g, h, s), flat(V[s])), (at(hs_g, h, s), flat(O[s]))])
            edge_loads(GCN1)
            for s in range(2):
                sp.wait_ge(s_sc[s], scat(GCN1, NG // 2 - 1))
            dense(1, lambda h, s, last: [(flat(DA[s]), at(hs_g, h, s)), (flat(DC[s]), at(tabA_g, h, s))],
                  lambda h, s, last: [(at(gt_g, h, s), flat(O[s]))])
            edge_loads(GCN2)
            for s in range(2):
                sp.wait_ge(s_sc[s], scat(GCN2, NG // 2 - 1))
            dense(2, lambda h, s, last: [(flat(DA[s]), at(gt_g, h, s)), (flat(DC[s]), at(tabA_g, h, s)), (flat(V[s]), at(x1_g, h, s))],
                  lambda h, s, last: [node_io(h, s, last, O[s], out_g, out_last)[::-1]])
            for s in range(2):
                sp.wait_ge(s_wr[2][s], 16 * (NG // 2))

        @block.gpsimd
        def _(pool):
            pool.memset(ident[:, :], 0.0).then_inc(s_const, 1)
            pool.memset(rev[:, :], 0.0).then_inc(s_const, 1)
            pool.wait_ge(s_const, 2)
            pool.affine_select(out=ident[:, :], in_=ident[:, :], compare_op=ALU.not_equal, fill=1.0,
                               base=0, pattern=[[-1, P]], channel_multiplier=1).then_inc(s_ident, 1)
            pool.affine_select(out=rev[:, :], in_=rev[:, :], compare_op=ALU.not_equal, fill=1.0,
                               base=-(P - 1), pattern=[[1, P]], channel_multiplier=1).then_inc(s_ident, 1)

            def edges(ph):
                table = {EC1: x, EC2: tabA, GCN1: hs, GCN2: gt}[ph]
                target = tabB if ph == EC2 else tabA
                width = CB if ph == EC2 else C

                def gather(h, s):
                    pool.wait_ge(s_gi[s], 16 * ((NG // 2) * ph + h + 1))
                    need(pool, s_xc if ph == EC1 else s_T, done(ph, h, s) - 2)
                    held(pool)
                    for k in range(K):
                        for side in range(2 if ph == EC1 else 1):
                            pool.indirect_dma_start(
                                out=G[s][:, k, side * C:(side + 1) * C], out_offset=None, in_=table[:, :],
                                in_offset=bass.IndirectOffsetOnAxis(ap=gi[s][:, side * K + k:side * K + k + 1], axis=0),
                            ).then_inc(s_g[s], 16)

                def scatter(h, s):
                    pool.wait_ge(s_si[s], 16 * ((NG // 2) * ph + h + 1))
                    pool.wait_ge(s_mt, done(ph, h, s))
                    held(pool)
                    for k in range(K):
                        pool.indirect_dma_start(
                            out=target[:, :], out_offset=bass.IndirectOffsetOnAxis(ap=si[s][:, k:k + 1], axis=0),
                            in_=MT[s][:, k, 0:width], in_offset=None, bounds_check=N - 1, oob_is_err=False,
                        ).then_inc(s_sc[s], 16)

                def step(h, s):
                    gather(h, s)
                    if not (isinstance(h, int) and h == 0):
                        scatter(h - 1, s)

                if ph == EC1:
                    gather(0, 0)
                    gather(0, 1)
                    pool.wait_ge(s_zA, 16 * ZA)
                    step(1, 0)
                    step(1, 1)
                    with pool.Fori(2, NG // 2) as h:
                        step(h, 0)
                        step(h, 1)
                else:
                    run(pool, step)
                scatter(NG // 2 - 1, 0)
                scatter(NG // 2 - 1, 1)
                for s in range(2):
                    pool.wait_ge(s_sc[s], scat(ph, NG // 2 - 1))

            edges(EC1)
            pool.wait_ge(s_zB, 16 * ZB)
            edges(EC2)

            pool.wait_ge(s_fold, 2)

            def shift(h, s):
                pool.wait_ge(s_ld[0][s], 32 * (h + 1))
                need(pool, s_x1, done(0, h, s) - 2)
                if not (isinstance(h, int) and h == 0):
                    pool.wait_ge(s_wr[0][s], 32 * h)
                pool.tensor_tensor(U[s][:, :, :], DB[s][:, :, 0:C], bnrow[:, 0:1, :].to_broadcast([P, R, C]), ALU.mult).then_inc(s_v, 1)
                pool.tensor_tensor(V[s][:, :, :], DA[s][:, :, :], bnrow[:, 1:2, :].to_broadcast([P, R, C]), ALU.add).then_inc(s_v, 1)

            run(pool, shift)
            for s in range(2):
                pool.wait_ge(s_wr[0][s], 32 * (NG // 2))
            edges(GCN1)
            for s in range(2):
                pool.wait_ge(s_wr[1][s], 16 * (NG // 2))
            edges(GCN2)

            def add_self(h, s):
                pool.wait_ge(s_ld[2][s], 48 * (h + 1))
                need(pool, s_f1, 2 * h + s - 1)
                pool.tensor_tensor(U[s][:, :, :], DA[s][:, :, :], DC[s][:, :, :], ALU.add).then_inc(s_f0, 1)

            run(pool, add_self)

        @block.scalar
        def _(act):
            def edges(ph):
                conv = ph in (EC1, EC2)
                width = CB if ph == EC2 else C

                def front(h, s):
                    n = done(ph, h, s)
                    if ph == EC1:
                        act.wait_ge(s_xc, n)
                        need(act, s_ssq, n - 1)
                        act.activation(sq[:, :, :], xc[:, :, :], ACT.Square).then_inc(s_sq, 1)
                        act.wait_ge(s_ssq, n)
                        need(act, s_rstd, n - 1)
                        act.activation(ln[:, 3, :], ln[:, 2, :], ACT.Sqrt, bias=eps[:, :], scale=1.0 / C).then_inc(s_std, 1)
                    act.wait_ge(s_T, n)
                    if conv:
                        need(act, s_u1, n - 2)
                        if ph == EC2:
                            need(act, s_back, n - 1 - NG)
                    else:
                        need(act, s_scan, n - 2)
                    p = P if conv else C
                    act.activation(TS[s][0:p, :], pT[0:p, :], ACT.Copy).then_inc(s_TS, 1)

                def result(h, s):
                    n = done(ph, h, s)
                    act.wait_ge(s_mT, n)
                    need(act, s_sc[s], scat(ph, h - 1))
                    if conv:
                        need(act, s_st, n - 2)
                    if ph == EC1 and not (isinstance(h, int) and h == 0):
                        act.wait_ge(s_ms[s], 16 * h)
                    act.activation(MT[s][:, :, 0:width], pBk[:, :, 0:width], ACT.Copy).then_inc(s_mt, 1)
                    if conv:
                        act.activation(MQ[s][:, :, :], pBk[:, :, 0:C], ACT.Square).then_inc(s_mq, 1)

                def step(h, s):
                    n = done(ph, h, s)
                    prev = (h, 0) if s == 1 else (h - 1, 1)
                    first = isinstance(h, int) and h == 0 and s == 0
                    front(h, s)
                    if conv:
                        act.wait_ge(s_u1, n)
                        need(act, s_u2, n - 1)
                        act.activation(A1[:, :], pU1[0:C, :], ACT.Relu,
                                       bias=cols[0:C, B1A:B1A + 1] if ph == EC1 else bias2[:, :]).then_inc(s_a1, 1)
                    if not first:
                        result(*prev)
                    if conv:
                        act.wait_ge(s_u2, n)
                        need(act, s_scan, n - 2)
                        b = B1B if ph == EC1 else B2B
                        act.activation(A2[s][:, :], pU2[0:C, :], ACT.Relu, bias=cols[0:C, b:b + 1]).then_inc(s_a2, 1)

                run(act, step)
                result(NG // 2 - 1, 1)

            act.wait_ge(s_zero, 1)
            wA = NP * C // P // ZA
            vA = tabA.rearrange("(z p r) c -> z p (r c)", z=ZA, p=P)
            vB = tabB.rearrange("(z p r) c -> z p (r c)", z=ZB, p=P)
            for z in range(ZA):
                act.dma_start(vA[z], zeros[:, 0:wA]).then_inc(s_zA, 16)
            for z in range(ZB):
                act.dma_start(vB[z], zeros[:, :]).then_inc(s_zB, 16)
            act.wait_ge(s_wts, 16 * 21)
            def deviation(steps):
                act.wait_ge(s_bn, steps)
                act.activation(bn[0:C, 4:5], bn[0:C, 3:4], ACT.Sqrt, bias=eps[0:C, :]).then_inc(s_bnsd, 1)

            edges(EC1)
            deviation(4)
            act.wait_ge(s_fold, 1)
            edges(EC2)
            deviation(8 + 5 + 2 + 4)

            def square(h, s):
                n = 2 * h + s + 1
                m = NG + n
                act.wait_ge(s_ld[0][s], 32 * (h + 1))
                need(act, s_dis, n - 2)
                act.activation(deg[s][:, :], DB[s][:, :, C:CB].rearrange("p r c -> p (r c)"), ACT.Sqrt, bias=ones[:, 0:1]).then_inc(s_deg, 1)
                act.wait_ge(s_xc, m)
                act.activation(sq[:, :, :], xc[:, :, :], ACT.Square).then_inc(s_dsq, 1)
                act.wait_ge(s_ssq, m)
                act.activation(ln[:, 3, :], ln[:, 2, :], ACT.Sqrt, bias=eps[:, :], scale=1.0 / C).then_inc(s_std, 1)

            run(act, square)
            edges(GCN1)

            def gcn_dense(h, s):
                n = 2 * h + s + 1
                act.wait_ge(s_zT, n)
                need(act, s_hm, n - 2)
                act.activation(TS[s][:, :], pT[:, :], ACT.Copy).then_inc(s_zTS, 1)
                act.wait_ge(s_hm, n)
                need(act, s_gm, n - 1)
                for half in range(2):
                    act.activation(HT[:, half, :], pH[half][:, :], ACT.Relu, bias=cols[:, GB1:GB1 + 1]).then_inc(s_hr, 1)

            run(act, gcn_dense)
            edges(GCN2)

        @block.vector
        def _(dve):
            dve.memset(raw[:, 0, :, :], 0)
            dve.memset(raw[:, 1:4, :, :], int(PAD)).then_inc(s_pad, 1)
            dve.memset(zeros[:, :], 0.0).then_inc(s_zero, 1)
            done_set = [0]

            def chain(ins):
                done_set[0] += 1
                ins.then_inc(s_set, 1)
                dve.wait_ge(s_set, done_set[0])

            chain(dve.memset(ones[:, :], 1.0))
            chain(dve.memset(eps[:, :], EPS))
            chain(dve.memset(acc[:, :], 0.0))
            dve.wait_ge(s_ident, 2)
            chain(dve.tensor_copy(ident16[:, :], ident[:, :]))
            chain(dve.tensor_copy(rev16[:, :], rev[:, :]))
            dve.wait_ge(s_raw, 16 * (3 * 3 + 5))
            SRC, DST, SE, SS, EQP, EQN, ME, MS, CUR, TMP = range(10)
            dve.tensor_copy(rows[:, SRC, :, :], raw[:, 0, :, :])
            chain(dve.tensor_copy(rows[:, CUR, :, :], raw[:, 1, :, :]))
            chain(dve.tensor_copy(rows[:, TMP, :, :], raw[:, 3, :, :]))
            chain(dve.tensor_tensor(rows[:, EQP, :, :], rows[:, CUR, :, :], rows[:, TMP, :, :], ALU.is_equal))
            chain(dve.tensor_copy(rows[:, TMP, :, :], raw[:, 2, :, :]))
            chain(dve.tensor_tensor(rows[:, EQN, :, :], rows[:, CUR, :, :], rows[:, TMP, :, :], ALU.is_equal))
            dve.tensor_scalar(rows[:, DST, :, :], rows[:, CUR, :, :], float(N - 1), None, ALU.min)
            dve.scalar_tensor_tensor(rows[:, SS, :, :], rows[:, EQP, :, :], PAD, rows[:, CUR, :, :], ALU.mult, ALU.add)
            chain(dve.scalar_tensor_tensor(rows[:, SE, :, :], rows[:, EQN, :, :], PAD, rows[:, CUR, :, :], ALU.mult, ALU.add))
            dve.tensor_scalar(rows[:, ME, :, :], rows[:, SE, :, :], float(N), None, ALU.is_lt)
            dve.tensor_scalar(rows[:, MS, :, :], rows[:, SS, :, :], float(N), None, ALU.is_lt).then_inc(s_rows, 1)
            dve.wait_ge(s_rowsT, 1)
            for t, o, a in ((gidx, 0, SRC), (gidx, K, DST), (sidx, 0, SE), (flags, 0, EQP), (flags, K, EQN), (masks, 0, ME)):
                dve.tensor_copy(t[:, :, o:o + K], bank[a][:, 0:NG * K].rearrange("p (g k) -> p g k", k=K))
            dve.tensor_copy(revrows[:, 0, :], bank[SS][:, :])
            dve.tensor_copy(revrows[:, 1, :], bank[MS][:, :]).then_inc(s_revrows, 1)
            dve.wait_ge(s_revT, 1)
            for j in range(K):
                for t, a in ((sidx, 0), (masks, 1)):
                    dve.tensor_copy(t[:, :, K + j:K + j + 1], bank[a][:, 0:NG * K].rearrange("p (g k) -> p g k", k=K)[:, :, K - 1 - j:K - j]).then_inc(s_set, 1)
            done_set[0] += 2 * K
            dve.wait_ge(s_set, done_set[0])
            dve.drain().then_inc(s_idx, 1)
            dve.wait_ge(s_wts, 16 * 21)
            for l in range(2):
                dve.tensor_tensor(Wc[l][C:P, :], Wc[l][C:P, :], Wtmp[C:P, l, :], ALU.subtract).then_inc(s_wcat, 1)

            def edges(ph):
                conv = ph in (EC1, EC2)
                fo = K if ph == EC2 else 0

                def front(h, s):
                    n = done(ph, h, s)
                    g = group(ph, h, s)
                    need(dve, s_flT, n - 2)
                    held(dve)
                    dve.tensor_copy(fl[s][:, :], flags[:, bass.ds(g, 1), fo:fo + K].rearrange("p a k -> p (a k)")).then_inc(s_fl, 1)
                    if conv:
                        need(dve, s_st, n - 2)
                        dve.tensor_copy(mk[s][:, :], masks[:, bass.ds(g, 1), fo:fo + K].rearrange("p a k -> p (a k)")).then_inc(s_mk, 1)
                    if ph == EC1:
                        rowsG = G[s][:, :, :].rearrange("p k (a c) -> p (k a) c", a=2)
                        rowsH = H[s][:, :, :].rearrange("p k (a c) -> p (k a) c", a=2)
                        dve.wait_ge(s_g[s], gath(ph, h))
                        dve.tensor_reduce(ln[:, 0, :], rowsG, AX, ALU.add).then_inc(s_sum, 1)
                        dve.wait_ge(s_sum, n)
                        dve.tensor_scalar(ln[:, 1, :], ln[:, 0, :], 1.0 / C, None, ALU.mult).then_inc(s_mean, 1)
                        dve.wait_ge(s_mean, n)
                        dve.tensor_tensor(xc[:, :, :], rowsG, ln[:, 1, :].unsqueeze(2).to_broadcast([P, 2 * K, C]), ALU.subtract).then_inc(s_xc, 1)
                        dve.wait_ge(s_sq, n)
                        dve.tensor_reduce(ln[:, 2, :], sq[:, :, :], AX, ALU.add).then_inc(s_ssq, 1)
                        dve.wait_ge(s_std, n)
                        dve.reciprocal(ln[:, 4, :], ln[:, 3, :]).then_inc(s_rstd, 1)
                        dve.wait_ge(s_rstd, n)
                        need(dve, s_T, n - 2)
                        dve.scalar_tensor_tensor(rowsH, xc[:, :, :], 0.0, ln[:, 4, :].unsqueeze(2).to_broadcast([P, 2 * K, C]), ALU.max, ALU.mult).then_inc(s_h, 1)
                    if ph == EC2:
                        first = isinstance(h, int) and h == 0 and s == 0
                        dve.wait_ge(s_TS, n)
                        dve.wait_ge(s_flT, n)
                        if not first:
                            dve.wait_ge(s_back, n - 1 - NG)
                        dve.tensor_tensor_scan(TS[s][C:P, :], pF[s][C:P, :], TS[s][C:P, :],
                                               0.0 if first else TS[1 - s][C:P, GE - 1:GE], ALU.mult, ALU.max).then_inc(s_back, 1)

                def scan(h, s):
                    n = done(ph, h, s)
                    first = isinstance(h, int) and h == 0 and s == 0
                    dve.wait_ge(s_flT, n)
                    need(dve, s_mT, n - 2)
                    need(dve, s_scan, n - 1)
                    if conv:
                        dve.wait_ge(s_a2, n)
                        data = A2[s][:, :]
                    else:
                        dve.wait_ge(s_TS, n)
                        data = TS[s][0:C, :]
                    if ph == EC2:
                        if not first:
                            dve.wait_ge(s_cnt, n - 1 - NG)
                        dve.tensor_tensor_scan(M[s][C:CB, :], pF[s][C:CB, :], ones[C:CB, :],
                                               0.0 if first else M[1 - s][C:CB, GE - 1:GE], ALU.mult, ALU.add).then_inc(s_cnt, 1)
                    dve.tensor_tensor_scan(M[s][0:C, :], pF[s][0:C, :], data,
                                           0.0 if first else M[1 - s][0:C, GE - 1:GE],
                                           ALU.mult, ALU.max if conv else ALU.add).then_inc(s_scan, 1)

                def add_stats(h, s):
                    n = done(ph, h, s)
                    dve.wait_ge(s_st, n)
                    need(dve, s_acc, n - 1)
                    dve.tensor_tensor(acc[:, :], acc[:, :], pS[s][0:C, 0:2], ALU.add).then_inc(s_acc, 1)

                def step(h, s):
                    front(h, s)
                    if conv:
                        if not (isinstance(h, int) and h == 0 and s == 0):
                            scan(*((h, 0) if s == 1 else (h - 1, 1)))
                        if not (isinstance(h, int) and h == 0):
                            add_stats(h - 1, s)
                    else:
                        scan(h, s)

                run(dve, step)
                if conv:
                    scan(NG // 2 - 1, 1)
                    add_stats(NG // 2 - 1, 0)
                    add_stats(NG // 2 - 1, 1)

            bn_steps = [0]

            def bn_chain(ins):
                bn_steps[0] += 1
                ins.then_inc(s_bn, 1)
                dve.wait_ge(s_bn, bn_steps[0])

            def batch_norm(ph, ga, be):
                dve.wait_ge(s_acc, NG * (ph + 1))
                b = lambda j: bn[0:C, j:j + 1]
                bn_chain(dve.tensor_scalar(bn[0:C, 0:2], acc[:, :], 1.0 / N, None, ALU.mult))
                bn_chain(dve.tensor_tensor(b(2), b(0), b(0), ALU.mult))
                bn_chain(dve.tensor_tensor(b(3), b(1), b(2), ALU.subtract))
                bn_chain(dve.tensor_scalar(b(3), b(3), 0.0, None, ALU.max))
                dve.wait_ge(s_bnsd, ph + 1)
                bn_chain(dve.reciprocal(b(4), b(4)))
                bn_chain(dve.tensor_tensor(b(5), b(4), cols[0:C, ga:ga + 1], ALU.mult))
                bn_chain(dve.tensor_tensor(b(6), b(0), b(5), ALU.mult))
                bn_chain(dve.tensor_tensor(b(7), cols[0:C, be:be + 1], b(6), ALU.subtract))

            edges(EC1)
            batch_norm(EC1, GA1, BE1)
            for t, j in ((a1, 5), (c1, 7)):
                bn_chain(dve.tensor_copy(t[0:C, :], bn[0:C, j:j + 1]))
                bn_chain(dve.tensor_copy(t[C:P, :], bn[0:C, j:j + 1]))
            bn_chain(dve.tensor_scalar(Weff[:, :], Wc[1][:, :], a1[:, :], None, ALU.mult))
            dve.wait_ge(s_bnp, 1)
            bn_chain(dve.tensor_tensor(bias2[:, :], pS[0][0:C, 8:9], cols[0:C, B2A:B2A + 1], ALU.add))
            bn_chain(dve.memset(acc[:, :], 0.0))
            dve.drain().then_inc(s_fold, 1)
            BN1_STEPS = bn_steps[0]
            edges(EC2)
            batch_norm(EC2, GA2, BE2)
            for j, c in ((0, 5), (1, 7)):
                bn_chain(dve.tensor_scalar(diag[:, j, :], ident[0:C, 0:C], bn[0:C, c:c + 1], None, ALU.mult))
            dve.wait_ge(s_bnp, 2)
            bn_chain(dve.tensor_copy(bnrow[:, :, :], pU1[:, 0:2 * C].rearrange("p (j c) -> p j c", j=2)))
            dve.drain().then_inc(s_fold, 1)

            def stream(h, s):
                n = 2 * h + s + 1
                m = NG + n
                d = dis[:, bass.ds(2 * h + s, 1), :].rearrange("p a r -> p (a r)")
                dve.wait_ge(s_v, 2 * n)
                dve.tensor_tensor(V[s][:, :, :], U[s][:, :, :], V[s][:, :, :], ALU.add).then_inc(s_x1, 1)
                dve.wait_ge(s_x1, n)
                dve.tensor_reduce(ln[:, 0, :], V[s][:, :, :], AX, ALU.add).then_inc(s_sum, 1)
                dve.wait_ge(s_deg, n)
                dve.reciprocal(d, deg[s][:, :]).then_inc(s_dis, 1)
                dve.wait_ge(s_sum, m)
                dve.tensor_scalar(ln[:, 1, :], ln[:, 0, :], 1.0 / C, None, ALU.mult).then_inc(s_mean, 1)
                dve.wait_ge(s_mean, m)
                dve.tensor_tensor(xc[:, :, :], V[s][:, :, :], ln[:, 1, :].unsqueeze(2).to_broadcast([P, R, C]), ALU.subtract).then_inc(s_xc, 1)
                dve.wait_ge(s_dsq, n)
                dve.tensor_reduce(ln[:, 2, :], sq[:, :, :], AX, ALU.add).then_inc(s_ssq, 1)
                dve.wait_ge(s_std, m)
                dve.reciprocal(ln[:, 4, :], ln[:, 3, :]).then_inc(s_rstd, 1)
                dve.wait_ge(s_rstd, m)
                dve.wait_ge(s_dis, n)
                dve.tensor_tensor(ln[:, 4, :], ln[:, 4, :], d, ALU.mult).then_inc(s_drs, 1)
                dve.wait_ge(s_drs, n)
                if not (isinstance(h, int) and h == 0):
                    dve.wait_ge(s_wr[0][s], 32 * h)
                dve.scalar_tensor_tensor(O[s][:, :, :], xc[:, :, :], 0.0, ln[:, 4, :].unsqueeze(2).to_broadcast([P, R, C]), ALU.max, ALU.mult).then_inc(s_o, 1)

            run(dve, stream)
            edges(GCN1)

            def dis_rows(h, s):
                return dis[:, bass.ds(2 * h + s, 1), :].rearrange("p a r -> p (a r)").unsqueeze(2).to_broadcast([P, R, C])

            def gcn_front(h, s):
                n = 2 * h + s + 1
                dve.wait_ge(s_ld[1][s], 32 * (h + 1))
                dve.tensor_tensor(U[s][:, :, :], DA[s][:, :, :], DC[s][:, :, :], ALU.add).then_inc(s_used, 1)
                dve.wait_ge(s_used, n)
                need(dve, s_zT, n - 2)
                dve.tensor_tensor(Z[s][:, :, :], U[s][:, :, :], dis_rows(h, s), ALU.mult).then_inc(s_z, 1)

            def gcn_back(h, s):
                n = 2 * h + s + 1
                dve.wait_ge(s_gm, n)
                if not (isinstance(h, int) and h == 0):
                    dve.wait_ge(s_wr[1][s], 16 * h)
                dve.tensor_tensor(O[s][:, :, :], pG[:, :].rearrange("p (r c) -> p r c", c=C), dis_rows(h, s), ALU.mult).then_inc(s_o, 1)

            def gcn_step(h, s):
                gcn_front(h, s)
                if not (isinstance(h, int) and h == 0 and s == 0):
                    gcn_back(*((h, 0) if s == 1 else (h - 1, 1)))

            run(dve, gcn_step)
            gcn_back(NG // 2 - 1, 1)
            edges(GCN2)

            def final(h, s):
                n = 2 * h + s + 1
                dve.wait_ge(s_f0, n)
                dve.tensor_tensor(Z[s][:, :, :], U[s][:, :, :], dis_rows(h, s), ALU.mult).then_inc(s_f1, 1)
                dve.wait_ge(s_f1, n)
                dve.tensor_tensor(Z[s][:, :, :], Z[s][:, :, :], gb2r[:, :].unsqueeze(1).to_broadcast([P, R, C]), ALU.add).then_inc(s_f2, 1)
                dve.wait_ge(s_f2, n)
                if not (isinstance(h, int) and h == 0):
                    dve.wait_ge(s_wr[2][s], 16 * h)
                dve.scalar_tensor_tensor(O[s][:, :, :], Z[s][:, :, :], 0.0, V[s][:, :, :], ALU.max, ALU.add).then_inc(s_o, 1)

            run(dve, final)

        @block.tensor
        def _(pe):
            pe.wait_ge(s_rows, 1)
            for a in range(8):
                for c in range(CH):
                    last = pe.transpose(bank[a][:, c * P:(c + 1) * P], rows[:, a, c, :], ident[:, :])
            last.then_inc(s_rowsT, 1)
            pe.wait_ge(s_revrows, 1)
            for a in range(2):
                last = pe.matmul(bank[a][:, :], rev[:, :], revrows[:, a, :], start=True, stop=True)
            last.then_inc(s_revT, 1)

            def edges(ph):
                conv = ph in (EC1, EC2)
                width = CB if ph == EC2 else C

                def front(h, s):
                    n = done(ph, h, s)
                    pe.wait_ge(s_fl, n)
                    need(pe, s_scan, n - 2)
                    for k in range(K):
                        t = K - 1 - k if ph == EC2 else k
                        last = pe.matmul(pF[s][:, k * P:(k + 1) * P], fl[s][:, t:t + 1].to_broadcast([P, P]),
                                         (rev16 if ph == EC2 else ident16)[:, :], start=True, stop=True)
                    last.then_inc(s_flT, 1)
                    need(pe, s_TS, n - 1)
                    if ph == EC1:
                        pe.wait_ge(s_h, n)
                        for k in range(K):
                            last = pe.transpose(pT[:, k * P:(k + 1) * P], H[s][:, k, :], ident[:, :])
                        last.then_inc(s_T, 1)
                    else:
                        pe.wait_ge(s_g[s], gath(ph, h))
                        if ph == EC2:
                            pe.wait_ge(s_ml[s], 16 * (h + 1))
                        held(pe)
                        for k in range(K):
                            if ph == EC2:
                                last = pe.matmul(pT[:, k * P:(k + 1) * P], G[s][:, K - 1 - k, :], rev[:, :], start=True, stop=True)
                            else:
                                last = pe.transpose(pT[0:C, k * P:(k + 1) * P], G[s][:, k, 0:C], ident[:, :])
                        last.then_inc(s_T, 1)

                def turn_result(h, s):
                    n = done(ph, h, s)
                    pe.wait_ge(s_scan, n)
                    need(pe, s_mt, n - 1)
                    if conv:
                        need(pe, s_mq, n - 1)
                    held(pe)
                    for k in range(K):
                        last = pe.transpose(pBk[:, k, 0:width], M[s][0:width, k * P:(k + 1) * P], ident[0:width, 0:width])
                    last.then_inc(s_mT, 1)

                def stats(h, s):
                    n = done(ph, h, s)
                    pe.wait_ge(s_mk, n)
                    pe.wait_ge(s_mq, n)
                    need(pe, s_acc, n - 2)
                    for j, t in enumerate((MT[s], MQ[s])):
                        for k in range(K):
                            last = pe.matmul(pS[s][0:C, j:j + 1], t[:, k, 0:C], mk[s][:, k:k + 1], start=k == 0, stop=k == K - 1)
                    last.then_inc(s_st, 1)

                def step(h, s):
                    n = done(ph, h, s)
                    first = isinstance(h, int) and h == 0 and s == 0
                    prev = (h, 0) if s == 1 else (h - 1, 1)
                    front(h, s)
                    if conv:
                        pe.wait_ge(s_TS, n)
                        if ph == EC2:
                            pe.wait_ge(s_back, n - NG)
                        need(pe, s_a1, n - 1)
                        pe.matmul(pU1[0:C, :], (Wc[0] if ph == EC1 else Weff)[:, :], TS[s][:, :], start=True, stop=True).then_inc(s_u1, 1)
                    if not first:
                        turn_result(*prev)
                    if conv:
                        pe.wait_ge(s_a1, n)
                        need(pe, s_a2, n - 1)
                        held(pe)
                        l = 0 if ph == EC1 else 1
                        pe.matmul(pU2[0:C, :], Wb[l][:, :], A1[:, :], start=True, stop=True).then_inc(s_u2, 1)
                        if not first:
                            stats(*prev)

                run(pe, step)
                turn_result(NG // 2 - 1, 1)
                if conv:
                    stats(NG // 2 - 1, 1)

            pe.wait_ge(s_wcat, 2)
            edges(EC1)
            pe.wait_ge(s_bn, 8 + 5)
            pe.matmul(pS[0][0:C, 8:9], Wc[1][:, :], c1[:, :], start=True, stop=True).then_inc(s_bnp, 1)
            pe.wait_ge(s_fold, 1)
            edges(EC2)
            pe.wait_ge(s_bn, 8 + 5 + 2 + 8 + 2)
            for j in range(2):
                last = pe.matmul(pU1[:, j * C:(j + 1) * C], ones[0:C, 0:P], diag[:, j, :], start=True, stop=True)
            last.then_inc(s_bnp, 1)
            edges(GCN1)

            def gcn_front(h, s):
                n = 2 * h + s + 1
                pe.wait_ge(s_z, n)
                need(pe, s_zTS, n - 1)
                for j in range(R // 2):
                    last = pe.transpose(pT[:, j * P:(j + 1) * P], Z[s][:, 2 * j:2 * j + 2, :].rearrange("p r c -> p (r c)"), ident[:, :])
                last.then_inc(s_zT, 1)

            def gcn_back(h, s):
                n = 2 * h + s + 1
                pe.wait_ge(s_hr, 2 * n)
                need(pe, s_o, ND + n - 1)
                for r in range(R):
                    last = pe.matmul(pG[:, r * C:(r + 1) * C], HT[:, r % 2, (r // 2) * P:(r // 2 + 1) * P], gw2[:, :], start=True, stop=True)
                last.then_inc(s_gm, 1)

            def gcn_step(h, s):
                n = 2 * h + s + 1
                gcn_front(h, s)
                if not (isinstance(h, int) and h == 0 and s == 0):
                    gcn_back(*((h, 0) if s == 1 else (h - 1, 1)))
                pe.wait_ge(s_zTS, n)
                need(pe, s_hr, 2 * n - 2)
                for half in range(2):
                    last = pe.matmul(pH[half][:, :], gw1[half * C:(half + 1) * C, :], TS[s][half * C:(half + 1) * C, :], start=True, stop=True)
                last.then_inc(s_hm, 1)

            run(pe, gcn_step)
            gcn_back(NG // 2 - 1, 1)
            edges(GCN2)


_INS = ["x", "src", "dst", "L0_gnn_W1a", "L0_gnn_b1a", "L0_gnn_W1b", "L0_gnn_b1b", "L0_gnn_gamma1", "L0_gnn_beta1",
        "L0_gnn_W2a", "L0_gnn_b2a", "L0_gnn_W2b", "L0_gnn_b2b", "L0_gnn_gamma2", "L0_gnn_beta2",
        "L1_gnn_W1", "L1_gnn_b1", "L1_gnn_W2", "L1_gnn_b2"]


def kernel(**inputs):
    import numpy as _np
    import concourse.bacc as _bacc
    from concourse import mybir as _mybir
    from concourse.bass_utils import run_bass_kernel_spmd as _run

    nc = _bacc.Bacc("TRN2", target_bir_lowering=False, num_devices=1)
    arrays, args = {}, []
    for name in _INS:
        a = _np.ascontiguousarray(inputs[name])
        arrays[f"in_{name}"] = a
        args.append(nc.dram_tensor(f"in_{name}", a.shape, _mybir.dt.from_np(a.dtype), kind="ExternalInput").ap())
    args.append(nc.dram_tensor("out_0", (N, C), F32, kind="ExternalOutput").ap())
    build(nc, *args)
    r = _run(nc, [arrays], core_ids=[0])
    return r.results[0]["out_0"]
```

```python
import concourse.bass as bass
import concourse.mybir as mybir
from concourse.alu_op_type import AluOpType as ALU
from contextlib import ExitStack


F32, BF16, I32 = mybir.dt.float32, mybir.dt.bfloat16, mybir.dt.int32
ACT = mybir.ActivationFunctionType
AX = mybir.AxisListType.X

P = 128
N, E, C, HID = 100000, 50000, 64, 128
K = 4
GE = K * P
TILES = -(-E // P)
NG = -(-TILES // (2 * K)) * 2
CH = 4
R = 8
GN = R * P
ND = -(-N // (2 * GN)) * 2
NP = ND * GN
LASTP = (N - (ND - 1) * GN) // R
CB = C + 1
PAD = float(2 ** 20)
EPS = 1e-5
ZA, ZA_FIRST, ZB = 28, 6, NG // 2
ZC = NP * C // P // ZA
assert (ND - 1) * GN < N and LASTP * R == N - (ND - 1) * GN and NG == ND
assert NP * C // P % ZA == 0 and NP // P % ZB == 0 and NP * CB // P // ZB <= ZC
assert CH * P >= NG * K and PAD > N

UNITS = (ND - 2) // 2
LAG = 4
RAW_LOADS = 3 * 3 + 5

EC1, EC2, GCN1, GCN2 = range(4)


def build(nc, x, src, dst, W1a, b1a, W1b, b1b, gamma1, beta1, W2a, b2a, W2b, b2b, gamma2, beta2,
          gW1, gb1, gW2, gb2, out):
    def dram(name, shape):
        return nc.dram_tensor(name, shape, F32, kind="Internal").ap()

    tabA = dram("tabA", (NP, C))
    tabB = dram("tabB", (NP, CB))
    m1e = dram("m1e", (NG * C, GE))
    x1 = dram("x1", (NP, C))
    hs = dram("hs", (NP, C))
    gt = dram("gt", (NP, C))

    def nodes(t, c=C):
        return t.rearrange("(g p r) c -> g p (r c)", p=P, r=R)

    m1e_g = m1e.rearrange("(g c) e -> g c e", c=C)
    tabA_g, tabB_g, x1_g, hs_g, gt_g = (nodes(t) for t in (tabA, tabB, x1, hs, gt))
    FULL = (ND - 1) * GN
    x_g, out_g = nodes(x[0:FULL, :]), nodes(out[0:FULL, :])
    x_last = x[FULL:N, :].rearrange("(p r) c -> p (r c)", r=R)
    out_last = out[FULL:N, :].rearrange("(p r) c -> p (r c)", r=R)

    with ExitStack() as ctx:
        def sb(name, shape, dt=F32):
            return ctx.enter_context(nc.sbuf_tensor(name, shape, dt))

        def sem(name):
            return ctx.enter_context(nc.semaphore(name))

        def two(name, shape, dt=F32):
            return [sb(f"{name}{s}", shape, dt) for s in range(2)]

        zeros = sb("zeros", [P, ZC])
        ident = sb("ident", [P, P])
        ident16 = sb("ident16", [P, P], BF16)
        ones = sb("ones", [P, GE])
        eps = sb("eps", [P, 1])
        raw = sb("raw", [P, 4, CH, P], I32)
        rows = sb("rows", [P, 10, CH, P])
        gidx = sb("gidx", [P, NG, 2 * K], I32)
        sidx = sb("sidx", [P, NG, 2 * K], I32)
        flags = sb("flags", [P, NG, 2 * K], BF16)
        masks = sb("masks", [P, NG, 2 * K])
        Wc = [sb(f"Wc{l}", [P, C]) for l in range(2)]
        Wtmp = sb("Wtmp", [P, 2, C])
        Weff = sb("Weff", [P, C])
        Wb = [sb(f"Wb{l}", [C, C]) for l in range(2)]
        cols = sb("cols", [P, 12])
        B1A, B1B, GA1, BE1, B2A, B2B, GA2, BE2, GB1 = range(9)
        gw1 = sb("gw1", [P, HID])
        gw2 = sb("gw2", [HID, C])
        gb2r = sb("gb2r", [P, C])
        acc = sb("acc", [1, 2, C])
        bn = sb("bn", [P, 8])
        a1, c1, bias2 = sb("a1", [P, 1]), sb("c1", [P, 1]), sb("bias2", [C, 1])
        diag = sb("diag", [C, 2, C])
        bnrow = sb("bnrow", [P, 2, C])
        gi, si = two("gi", [P, 2 * K], I32), two("si", [P, K], I32)
        fl, mk = two("fl", [P, K], BF16), two("mk", [P, K])
        G = two("G", [P, K, 2 * C])
        MF = two("MF", [P, GE])
        xc, sq = two("xc", [P, 2 * K, C]), two("sq", [P, 2 * K, C])
        H = two("H", [P, K, 2 * C])
        ln = two("ln", [P, 5, R])
        TS = two("TS", [P, GE])
        A1 = sb("A1", [C, GE])
        A2 = two("A2", [C, GE])
        M = two("M", [CB, GE])
        MT = two("MT", [P, K, 2, CB])
        dis = sb("dis", [P, ND, R])
        deg = two("deg", [P, R])
        DA, DB, DC = two("DA", [P, R, C]), two("DB", [P, R, CB]), two("DC", [P, R, C])
        U, V = two("U", [P, R, C]), two("V", [P, R, C])
        Z, O = two("Z", [P, R, C]), two("O", [P, R, C])
        ZT = two("ZT", [P, GE])
        HT = sb("HT", [P, 2, GE])
        iota_i = sb("iota_i", [P, 3, NG], I32)
        steps = sb("steps", [P, 3, NG])
        below = sb("below", [P, NG])
        missing = sb("missing", [P, 2])
        ready = sb("ready", [P, NG])
        units = sb("units", [1, 2, NG + 1])
        plan = sb("plan", [1, NG + 1], I32)

        bank = [ctx.enter_context(nc.psum_tensor(f"bank{b}", [P, GE], F32)) for b in range(8)]
        pT, pU1, pU2, pB, pS = bank[0], bank[3], bank[4], bank[5], [bank[6], bank[7]]
        pF = [bank[1], bank[2]]
        pBk = pB[:, 0:K * CB].rearrange("p (k c) -> p k c", c=CB)
        pFg, pZT, pH, pG = bank[1], [bank[2], bank[3]], [bank[4], bank[6]], bank[7]

        s_held = sem("held")
        s_const, s_ident, s_zero = sem("const_built"), sem("ident_ready"), sem("zero_ready")
        s_raw, s_wts, s_pad = sem("raw_loaded"), sem("weights_loaded"), sem("pad_written")
        s_zA, s_zB = sem("tabA_cleared"), sem("tabB_cleared")
        s_rows, s_rowsT, s_idx = (sem(n) for n in (
            "rows_ready", "rows_turned", "indices_ready"))
        s_iota, s_last, s_ready, s_avail, s_plan = (sem(n) for n in (
            "iota_ready", "last_dst_spread", "ready_marked", "ready_counted", "plan_ready"))
        s_wcat, s_set = sem("weights_stacked"), sem("setup_step")
        s_gi, s_si = [sem(f"gather_idx{s}") for s in range(2)], [sem(f"scatter_idx{s}") for s in range(2)]
        s_g, s_sc = [sem(f"gathered{s}") for s in range(2)], [sem(f"scattered{s}") for s in range(2)]
        s_ml, s_ms = [sem(f"m1e_loaded{s}") for s in range(2)], [sem(f"m1e_stored{s}") for s in range(2)]
        s_fl, s_mk, s_flT = sem("flags_staged"), sem("masks_staged"), sem("flags_spread")
        s_sum, s_mean, s_xc, s_sq, s_ssq, s_std, s_rstd, s_h = (sem(n) for n in (
            "ln_sum", "ln_mean", "ln_centred", "ln_squared", "ln_sumsq", "ln_std", "ln_rstd", "ln_out"))
        s_T, s_TS, s_back = sem("turned"), sem("turned_copied"), sem("dst_spread")
        s_u1, s_a1, s_u2, s_a2 = sem("layer1_sum"), sem("layer1_out"), sem("layer2_sum"), sem("layer2_out")
        s_scan, s_cnt, s_mT, s_mt, s_mq = (sem(n) for n in (
            "scanned", "counted", "result_turned", "result_copied", "result_squared"))
        s_st, s_acc = sem("stats_sum"), sem("stats_added")
        s_bnc = sem("bn_columns")
        s_bn, s_bnsd, s_bnp, s_fold = sem("bn_step"), sem("bn_std"), sem("bn_product"), sem("bn_folded")
        s_ld = [[sem(f"dense_loaded{ph}{s}") for s in range(2)] for ph in range(3)]
        s_wr = [[sem(f"dense_stored{ph}{s}") for s in range(2)] for ph in range(3)]
        s_x1w = [sem(f"x1_stored{s}") for s in range(2)]
        s_v, s_x1, s_used, s_o = sem("dense_shifted"), sem("stream_ready"), sem("dense_used"), sem("dense_out")
        s_deg, s_dis, s_dsq, s_drs = sem("degree_root"), sem("dis_ready"), sem("dense_squared"), sem("dense_rstd")
        s_z0, s_z, s_zT, s_zTS = sem("agg_added"), sem("agg_scaled"), sem("agg_turned"), sem("agg_copied")
        s_hm, s_hr, s_gm = sem("hidden_sum"), sem("hidden_out"), sem("gcn_product")
        s_credit = 2
        s_f0, s_f1, s_f2 = sem("final_added"), sem("final_scaled"), sem("final_biased")

        def need(eng, s, value):
            if not (isinstance(value, int) and value <= 0):
                eng.wait_ge(s, value)

        def held(eng):
            eng.sem_inc(s_held, 1)

        def run(eng, step, last=None):
            for h in range(2):
                step(h, 0)
                step(h, 1)
            if last is None:
                with eng.Fori(2, NG // 2) as h:
                    step(h, 0)
                    step(h, 1)
            else:
                with eng.Fori(2, NG // 2 - 1) as h:
                    step(h, 0)
                    step(h, 1)
                step(NG // 2 - 1, 0)
                last(NG // 2 - 1, 1)

        def done(ph, h, s):
            return NG * ph + 2 * h + s + 1

        def gath(ph, h):
            before = 0 if ph == EC1 else 16 * K * (NG // 2) * (ph + 1)
            return before + 16 * K * (2 if ph == EC1 else 1) * (h + 1)

        def scat(ph, h):
            return 16 * K * ((NG // 2) * ph + h + 1)

        def at(t, h, s):
            return t[bass.ds(2 * h + s, 1), :, :].rearrange("a p f -> p (a f)")

        def flat(t):
            return t[:, :, :].rearrange("p r c -> p (r c)")

        def node_io(h, s, last, tile, whole, part):
            if last:
                return flat(tile)[0:LASTP, :], part
            return flat(tile), at(whole, h, s)

        def group(ph, h, s):
            return 2 * h + s if ph == EC1 else (NG - 1 - s) - 2 * h

        def node_group(v, j):
            if isinstance(v, int) and v == UNITS:
                return 0 if j else ND - 1
            return (ND - 2 - j) - 2 * v

        def rows_of(t, g):
            return t[bass.ds(g, 1), :, :].rearrange("a p f -> p (a f)")

        def plan_at(eng, h, s):
            q = 2 * h + s
            if isinstance(q, int) and q < LAG:
                return None
            before = eng.value_load(plan[0:1, bass.ds(q, 1)], min_val=0, max_val=UNITS - 1)
            after = eng.value_load(plan[0:1, bass.ds(q + 1, 1)], min_val=0, max_val=UNITS)
            return before, after

        def if_planned(eng, at_step, unit):
            if at_step is not None:
                before, after = at_step
                with eng.If(after > before):
                    unit(before)

        def planned(eng, h, s, unit):
            if_planned(eng, plan_at(eng, h, s), unit)

        def remaining(eng, unit):
            first = eng.value_load(plan[0:1, NG:NG + 1], min_val=0, max_val=UNITS)
            with eng.If(first < UNITS):
                with eng.Fori(first, UNITS) as v:
                    unit(v)
            unit(UNITS)

        block = ctx.enter_context(nc.Block())

        @block.sync
        def _(sp):
            sp.wait_ge(s_pad, 1)
            W = P * (CH - 1)
            T6 = E // P - W
            rest = E - (E // P) * P

            def load_rows(a, v, shift):
                last = rest - max(shift, 0)
                if shift >= 0:
                    full = v[shift:shift + W * P].rearrange("(c t e) -> t c e", t=P, e=P)
                    sp.dma_start(raw[:, a, 0:CH - 1, :], full).then_inc(s_raw, 16)
                else:
                    sp.dma_start(raw[0:1, a, 0, 1:P], v[0:P - 1].rearrange("(t e) -> t e", t=1)).then_inc(s_raw, 16)
                    sp.dma_start(raw[1:P, a, 0, :], v[P - 1:P - 1 + (P - 1) * P].rearrange("(t e) -> t e", e=P)).then_inc(s_raw, 16)
                    sp.dma_start(raw[:, a, 1:CH - 1, :], v[P * P - 1:W * P - 1].rearrange("(c t e) -> t c e", t=P, e=P)).then_inc(s_raw, 16)
                b = W * P + shift
                sp.dma_start(raw[0:T6, a, CH - 1, :], v[b:b + T6 * P].rearrange("(t e) -> t e", e=P)).then_inc(s_raw, 16)
                b += T6 * P
                sp.dma_start(raw[T6:T6 + 1, a, CH - 1, 0:last], v[b:b + last].rearrange("(t e) -> t e", t=1)).then_inc(s_raw, 16)

            load_rows(0, src, 0)
            load_rows(1, dst, 0)
            load_rows(2, dst, 1)
            load_rows(3, dst, -1)
            sp.wait_ge(s_idx, 8)

            def stage(ph, h, s, back):
                need(sp, s_g[s], gath(ph, h - 1) if not (isinstance(h, int) and h == 0 and ph == EC1) else 0)
                held(sp)
                n = 2 * K if ph == EC1 else K
                sp.dma_start(gi[s][:, 0:n], gidx[:, bass.ds(group(ph, h, s), 1), 0:n].rearrange("p a n -> p (a n)")).then_inc(s_gi[s], 16)

            def stage_scatter(ph, h, s):
                need(sp, s_sc[s], scat(ph, h - 1))
                held(sp)
                o = 0 if ph == EC1 else K
                sp.dma_start(si[s][:, :], sidx[:, bass.ds(group(ph, h, s), 1), o:o + K].rearrange("p a n -> p (a n)")).then_inc(s_si[s], 16)

            def edge_loads(ph, unit=None):
                def step(h, s):
                    stage(ph, h, s, 0)
                    if ph == EC1 and s == 1:
                        sp.dma_start(vB[bass.ds(h, 1), :, :].rearrange("a p f -> p (a f)"), zeros[:, 0:NP * CB // P // ZB]).then_inc(s_zB, 16)
                    if ph == EC2:
                        need(sp, s_back, done(ph, h, s) - 2 - NG)
                        sp.dma_start(MF[s][C:P, :], m1e_g[bass.ds(group(ph, h, s), 1), :, :].rearrange("a c e -> c (a e)")).then_inc(s_ml[s], 16)
                    if not (isinstance(h, int) and h == 0):
                        tail(ph, h - 1, s)
                    if ph == EC1 and isinstance(h, int) and (h, s) == (0, 1):
                        load_weights()
                    if unit:
                        planned(sp, h, s, unit)

                def tail(ph, h, s):
                    stage_scatter(ph, h, s)
                    if ph == EC1:
                        sp.wait_ge(s_scan, done(ph, h, s))
                        sp.dma_start(m1e_g[bass.ds(group(ph, h, s), 1), :, :].rearrange("a c e -> c (a e)"), M[s][0:C, :]).then_inc(s_ms[s], 16)

                run(sp, step)
                tail(ph, NG // 2 - 1, 0)
                tail(ph, NG // 2 - 1, 1)

            def load_weights():
                for l, (wa, wb) in enumerate(((W1a, W1b), (W2a, W2b))):
                    sp.dma_start(Wc[l][0:C, :], wa[C:2 * C, :]).then_inc(s_wts, 16)
                    sp.dma_start(Wc[l][C:P, :], wa[0:C, :]).then_inc(s_wts, 16)
                    sp.dma_start(Wtmp[C:P, l, :], wa[C:2 * C, :]).then_inc(s_wts, 16)
                    sp.dma_start(Wb[l][:, :], wb[:, :]).then_inc(s_wts, 16)
                for j, v in ((B1A, b1a), (B1B, b1b), (GA1, gamma1), (BE1, beta1), (B2A, b2a), (B2B, b2b),
                             (GA2, gamma2), (BE2, beta2), (GB1, gb1)):
                    sp.dma_start(cols[0:v.shape[0], j:j + 1], v.rearrange("(p a) -> p a", a=1)).then_inc(s_wts, 16)
                sp.dma_start(gw1[0:C, :], gW1[:, :]).then_inc(s_wts, 16)
                sp.dma_start(gw1[C:P, :], gW1[:, :]).then_inc(s_wts, 16)
                sp.dma_start(gw2[:, :], gW2[:, :]).then_inc(s_wts, 16)
                sp.dma_start(gb2r[:, :], gb2.rearrange("(a c) -> a c", a=1).to_broadcast([P, C])).then_inc(s_wts, 16)

            sp.wait_ge(s_zero, 1)
            vB = tabB.rearrange("(z p r) c -> z p (r c)", z=ZB, p=P)
            edge_loads(EC1)
            for s in range(2):
                sp.wait_ge(s_ms[s], 16 * (NG // 2))
            edge_loads(EC2)
            for s in range(2):
                sp.wait_ge(s_sc[s], scat(EC2, NG // 2 - 1))

            def stream_loads(h, s, last=False):
                if not (isinstance(h, int) and h == 0):
                    sp.wait_ge(s_dis, 2 * h + s - 1)
                tile, rows = node_io(h, s, last, DA[s], x_g, x_last)
                sp.dma_start(tile, rows).then_inc(s_ld[0][s], 16)
                sp.dma_start(flat(DB[s]), at(tabB_g, h, s)).then_inc(s_ld[0][s], 16)

            run(sp, stream_loads, lambda h, s: stream_loads(h, s, True))

            def gcn_loads(v):
                for j in range(2):
                    sp.wait_ge(s_used, 2 * v + j - 1 + s_credit)
                    held(sp)
                    for t, d in ((DA, hs_g), (DC, tabA_g)):
                        sp.dma_start(flat(t[j]), rows_of(d, node_group(v, j))).then_inc(s_ld[1][j], 16)

            def final_loads(v):
                for j in range(2):
                    sp.wait_ge(s_o, 2 * ND + 2 * v + j - 1)
                    held(sp)
                    for t, d in ((DA, gt_g), (DC, tabA_g), (V, x1_g)):
                        sp.dma_start(flat(t[j]), rows_of(d, node_group(v, j))).then_inc(s_ld[2][j], 16)

            sp.wait_ge(s_plan, 1)
            edge_loads(GCN1, gcn_loads)
            for s in range(2):
                sp.wait_ge(s_sc[s], scat(GCN1, NG // 2 - 1))
            remaining(sp, gcn_loads)
            for s in range(2):
                sp.wait_ge(s_x1w[s], 16 * (NG // 2))
                sp.wait_ge(s_wr[1][s], 16 * (UNITS + 2))
            edge_loads(GCN2, final_loads)
            for s in range(2):
                sp.wait_ge(s_sc[s], scat(GCN2, NG // 2 - 1))
            remaining(sp, final_loads)
            for s in range(2):
                sp.wait_ge(s_wr[2][s], 16 * (UNITS + 2))

        @block.gpsimd
        def _(pool):
            pool.iota(iota_i[:, 0, :], pattern=[[1, NG]], base=0, channel_multiplier=0).then_inc(s_iota, 1)
            pool.iota(iota_i[:, 1, :].rearrange("p (h s) -> p h s", s=2), pattern=[[1, NG // 2], [1, 2]], base=-1, channel_multiplier=0).then_inc(s_iota, 1)
            pool.iota(iota_i[:, 2, :], pattern=[[0, NG]], base=(ND - 3) * GN, channel_multiplier=-2 * GN).then_inc(s_iota, 1)
            pool.memset(ident[:, :], 0.0).then_inc(s_const, 1)
            pool.wait_ge(s_const, 1)
            pool.affine_select(out=ident[:, :], in_=ident[:, :], compare_op=ALU.not_equal, fill=1.0,
                               base=0, pattern=[[-1, P]], channel_multiplier=1).then_inc(s_ident, 1)

            def edges(ph):
                table = {EC1: x, EC2: tabA, GCN1: hs, GCN2: gt}[ph]
                target = tabB if ph == EC2 else tabA
                width = CB if ph == EC2 else C

                def gather(h, s):
                    pool.wait_ge(s_gi[s], 16 * ((NG // 2) * ph + h + 1))
                    need(pool, s_xc if ph == EC1 else s_T, done(ph, h, s) - 2)
                    held(pool)
                    for k in range(K):
                        for side in range(2 if ph == EC1 else 1):
                            pool.indirect_dma_start(
                                out=G[s][:, k, side * C:(side + 1) * C], out_offset=None, in_=table[:, :],
                                in_offset=bass.IndirectOffsetOnAxis(ap=gi[s][:, side * K + k:side * K + k + 1], axis=0),
                            ).then_inc(s_g[s], 16)

                def scatter(h, s):
                    pool.wait_ge(s_si[s], 16 * ((NG // 2) * ph + h + 1))
                    pool.wait_ge(s_mt, done(ph, h, s))
                    held(pool)
                    for k in range(K):
                        pool.indirect_dma_start(
                            out=target[:, :], out_offset=bass.IndirectOffsetOnAxis(ap=si[s][:, k:k + 1], axis=0),
                            in_=MT[s][:, k, 0, 0:width], in_offset=None, bounds_check=N - 1, oob_is_err=False,
                        ).then_inc(s_sc[s], 16)

                def step(h, s):
                    gather(h, s)
                    if not (isinstance(h, int) and h == 0):
                        scatter(h - 1, s)

                if ph == EC1:
                    gather(0, 0)
                    gather(0, 1)
                    pool.wait_ge(s_zA, 16 * ZA)
                    step(1, 0)
                    step(1, 1)
                    with pool.Fori(2, NG // 2) as h:
                        step(h, 0)
                        step(h, 1)
                else:
                    run(pool, step)
                scatter(NG // 2 - 1, 0)
                scatter(NG // 2 - 1, 1)
                for s in range(2):
                    pool.wait_ge(s_sc[s], scat(ph, NG // 2 - 1))

            edges(EC1)
            pool.wait_ge(s_zB, 16 * ZB)
            edges(EC2)

            pool.wait_ge(s_fold, 2)

            def shift(h, s):
                pool.wait_ge(s_ld[0][s], 32 * (h + 1))
                need(pool, s_x1, done(0, h, s) - 2)
                pool.tensor_tensor(U[s][:, :, :], DB[s][:, :, 0:C], bnrow[:, 0:1, :].to_broadcast([P, R, C]), ALU.mult).then_inc(s_v, 1)
                pool.tensor_tensor(V[s][:, :, :], DA[s][:, :, :], bnrow[:, 1:2, :].to_broadcast([P, R, C]), ALU.add).then_inc(s_v, 1)

            run(pool, shift)
            for s in range(2):
                pool.wait_ge(s_wr[0][s], 16 * (NG // 2))
            edges(GCN1)
            for s in range(2):
                pool.wait_ge(s_wr[1][s], 16 * (UNITS + 2))
            edges(GCN2)

        @block.scalar
        def _(act):
            def edges(ph, unit=None):
                conv = ph in (EC1, EC2)
                width = CB if ph == EC2 else C

                def front(h, s):
                    n = done(ph, h, s)
                    if ph == EC1:
                        act.wait_ge(s_xc, n)
                        need(act, s_ssq, n - 2)
                        act.activation(sq[s][:, :, :], xc[s][:, :, :], ACT.Square).then_inc(s_sq, 1)
                        act.wait_ge(s_ssq, n)
                        act.activation(ln[s][:, 3, :], ln[s][:, 2, :], ACT.Sqrt, bias=eps[:, :], scale=1.0 / C).then_inc(s_std, 1)
                    act.wait_ge(s_T, n)
                    if conv:
                        need(act, s_u1, n - 2)
                    else:
                        need(act, s_scan, n - 2)
                    p = P if ph == EC1 else C
                    act.activation(TS[s][0:p, :], pT[0:p, :], ACT.Copy).then_inc(s_TS, 1)

                def result(h, s):
                    n = done(ph, h, s)
                    act.wait_ge(s_mT, n)
                    need(act, s_sc[s], scat(ph, h - 1))
                    if conv:
                        need(act, s_st, n - 2)
                    act.activation(MT[s][:, :, 0, 0:width], pBk[:, :, 0:width], ACT.Copy).then_inc(s_mt, 1)
                    if conv:
                        act.activation(MT[s][:, :, 1, 0:C], pBk[:, :, 0:C], ACT.Square).then_inc(s_mq, 1)

                def layer1(h, s):
                    n = done(ph, h, s)
                    act.wait_ge(s_u1, n)
                    need(act, s_u2, n - 1)
                    act.activation(A1[:, :], pU1[0:C, :], ACT.Relu,
                                   bias=cols[0:C, B1A:B1A + 1] if ph == EC1 else bias2[:, :]).then_inc(s_a1, 1)

                def layer2(h, s):
                    n = done(ph, h, s)
                    act.wait_ge(s_u2, n)
                    need(act, s_scan, n - 2)
                    b = B1B if ph == EC1 else B2B
                    act.activation(A2[s][:, :], pU2[0:C, :], ACT.Relu, bias=cols[0:C, b:b + 1]).then_inc(s_a2, 1)

                def step(h, s):
                    first = isinstance(h, int) and h == 0 and s == 0
                    prev = (h, 0) if s == 1 else (h - 1, 1)
                    front(h, s)
                    if conv and not first:
                        layer2(*prev)
                    if conv:
                        layer1(h, s)
                    if not first:
                        result(*prev)
                    if unit:
                        planned(act, h, s, unit)

                run(act, step)
                if conv:
                    layer2(NG // 2 - 1, 1)
                result(NG // 2 - 1, 1)

            act.wait_ge(s_zero, 1)
            act.wait_ge(s_raw, 16 * RAW_LOADS)
            wA = NP * C // P // ZA
            vA = tabA.rearrange("(z p r) c -> z p (r c)", z=ZA, p=P)
            for z in range(ZA):
                if z == ZA_FIRST:
                    for s in range(2):
                        act.wait_ge(s_gi[s], 16)
                act.dma_start(vA[z], zeros[:, 0:wA]).then_inc(s_zA, 16)
            act.wait_ge(s_wts, 16 * 21)
            def deviation(steps):
                act.wait_ge(s_bn, steps)
                act.activation(bn[0:C, 4:5], bn[0:C, 3:4], ACT.Sqrt, bias=eps[0:C, :]).then_inc(s_bnsd, 1)

            edges(EC1)
            deviation(4)
            act.wait_ge(s_fold, 1)
            edges(EC2)
            deviation(8 + 5 + 2 + 4)

            def prev_of(h, s):
                return (h, 0) if s == 1 else (h - 1, 1)

            def deviation_rows(h, s):
                act.wait_ge(s_ssq, NG + 2 * h + s + 1)
                act.activation(ln[s][:, 3, :], ln[s][:, 2, :], ACT.Sqrt, bias=eps[:, :], scale=1.0 / C).then_inc(s_std, 1)

            def normal_rows(h, s):
                act.wait_ge(s_drs, 2 * h + s + 1)
                if not (isinstance(h, int) and h == 0):
                    act.wait_ge(s_wr[0][s], 16 * h)
                for r in range(R):
                    last = act.activation(O[s][:, r, :], xc[s][:, r, :], ACT.Relu, scale=ln[s][:, 4, r:r + 1])
                last.then_inc(s_o, 1)

            def store_hs(h, s):
                act.wait_ge(s_o, 2 * h + s + 1)
                act.dma_start(at(hs_g, h, s), flat(O[s])).then_inc(s_wr[0][s], 16)

            def stream(h, s):
                n = 2 * h + s + 1
                first = isinstance(h, int) and h == 0 and s == 0
                if not first:
                    deviation_rows(*prev_of(h, s))
                act.wait_ge(s_ld[0][s], 32 * (h + 1))
                need(act, s_dis, n - 2)
                act.activation(deg[s][:, :], DB[s][:, :, C:CB].rearrange("p r c -> p (r c)"), ACT.Sqrt, bias=ones[:, 0:1]).then_inc(s_deg, 1)
                act.wait_ge(s_x1, n)
                act.dma_start(at(x1_g, h, s), flat(Z[s])).then_inc(s_x1w[s], 16)
                if not first:
                    normal_rows(*prev_of(h, s))
                act.wait_ge(s_xc, NG + n)
                act.activation(sq[s][:, :, :], xc[s][:, :, :], ACT.Square).then_inc(s_dsq, 1)
                if not first:
                    store_hs(*prev_of(h, s))

            run(act, stream)
            deviation_rows(NG // 2 - 1, 1)
            normal_rows(NG // 2 - 1, 1)
            store_hs(NG // 2 - 1, 1)

            def gcn_unit(v):
                n = lambda j: 2 * v + j + 1 + s_credit
                for j in range(2):
                    act.wait_ge(s_zT, n(j))
                    act.wait_ge(s_hm, 2 * (n(j) - 2))
                    act.activation(ZT[j][:, :], pZT[j][:, :], ACT.Copy).then_inc(s_zTS, 1)
                for j in range(2):
                    act.wait_ge(s_gm, n(j) - 1)
                    for half in range(2):
                        act.wait_ge(s_hm, 2 * n(j) - 1 + half)
                        act.activation(HT[:, half, :], pH[half][:, :], ACT.Relu, bias=cols[:, GB1:GB1 + 1]).then_inc(s_hr, 1)
                for j in range(2):
                    act.wait_ge(s_o, ND + 2 * v + j + 1)
                    act.dma_start(rows_of(gt_g, node_group(v, j)), flat(O[j])).then_inc(s_wr[1][j], 16)

            def final_unit(v):
                for j in range(2):
                    act.wait_ge(s_o, 2 * ND + 2 * v + j + 1)
                    if isinstance(v, int) and j == 0:
                        act.dma_start(out_last, flat(O[j])[0:LASTP, :]).then_inc(s_wr[2][j], 16)
                    else:
                        act.dma_start(rows_of(out_g, node_group(v, j)), flat(O[j])).then_inc(s_wr[2][j], 16)

            act.sem_inc(s_zTS, s_credit)
            act.sem_inc(s_hr, 2 * s_credit)
            for s in range(2):
                act.sem_inc(s_wr[1][s], 16)
                act.sem_inc(s_wr[2][s], 16)
            act.wait_ge(s_plan, 1)
            edges(GCN1, gcn_unit)
            remaining(act, gcn_unit)
            edges(GCN2, final_unit)
            remaining(act, final_unit)

        @block.vector
        def _(dve):
            dve.memset(raw[:, 0, :, :], 0)
            dve.memset(raw[:, 1:4, :, :], int(PAD)).then_inc(s_pad, 1)
            dve.memset(zeros[:, :], 0.0).then_inc(s_zero, 1)
            done_set = [0]

            def chain(ins):
                done_set[0] += 1
                ins.then_inc(s_set, 1)
                dve.wait_ge(s_set, done_set[0])

            chain(dve.memset(ones[:, :], 1.0))
            chain(dve.memset(eps[:, :], EPS))
            chain(dve.memset(acc[:, :, :], 0.0))
            dve.wait_ge(s_ident, 1)
            chain(dve.tensor_copy(ident16[:, :], ident[:, :]))
            dve.wait_ge(s_raw, 16 * RAW_LOADS)
            SRC, DST, SE, SS, EQP, EQN, ME, MS, CUR, TMP = range(10)
            dve.tensor_copy(rows[:, SRC, :, :], raw[:, 0, :, :])
            chain(dve.tensor_copy(rows[:, CUR, :, :], raw[:, 1, :, :]))
            chain(dve.tensor_copy(rows[:, TMP, :, :], raw[:, 3, :, :]))
            chain(dve.tensor_tensor(rows[:, EQP, :, :], rows[:, CUR, :, :], rows[:, TMP, :, :], ALU.is_equal))
            chain(dve.tensor_copy(rows[:, TMP, :, :], raw[:, 2, :, :]))
            chain(dve.tensor_tensor(rows[:, EQN, :, :], rows[:, CUR, :, :], rows[:, TMP, :, :], ALU.is_equal))
            dve.tensor_scalar(rows[:, DST, :, :], rows[:, CUR, :, :], float(N - 1), None, ALU.min)
            dve.scalar_tensor_tensor(rows[:, SS, :, :], rows[:, EQP, :, :], PAD, rows[:, CUR, :, :], ALU.mult, ALU.add)
            chain(dve.scalar_tensor_tensor(rows[:, SE, :, :], rows[:, EQN, :, :], PAD, rows[:, CUR, :, :], ALU.mult, ALU.add))
            dve.tensor_scalar(rows[:, ME, :, :], rows[:, SE, :, :], float(N), None, ALU.is_lt)
            dve.tensor_scalar(rows[:, MS, :, :], rows[:, SS, :, :], float(N), None, ALU.is_lt).then_inc(s_rows, 1)
            dve.wait_ge(s_rowsT, 1)
            turned = ((gidx, 0, SRC), (gidx, K, DST), (sidx, 0, SE), (sidx, K, SS),
                      (flags, 0, EQP), (flags, K, EQN), (masks, 0, ME), (masks, K, MS))
            for t, o, a in turned:
                dve.tensor_copy(t[:, :, o:o + K], bank[a][:, 0:NG * K].rearrange("p (g k) -> p g k", k=K)).then_inc(s_idx, 1)
            dve.wait_ge(s_idx, len(turned))
            dve.wait_ge(s_iota, 3)
            chain(dve.tensor_copy(steps[:, :, :], iota_i[:, :, :]))
            dve.wait_ge(s_last, 1)
            chain(dve.tensor_scalar(below[:, :], bank[0][:, K - 1:NG * K:K], steps[:, 2, 0:1], None, ALU.is_lt))
            chain(dve.tensor_reduce(missing[:, 0:1], below[:, :], AX, ALU.add))
            chain(dve.tensor_scalar(missing[:, 1:2], missing[:, 0:1], -1.0, float(NG - 1 + LAG), ALU.mult, ALU.add))
            dve.tensor_scalar(ready[:, :], steps[:, 0, :], missing[:, 1:2], None, ALU.is_ge).then_inc(s_ready, 1)
            dve.wait_ge(s_avail, 1)
            chain(dve.tensor_tensor(units[:, 0, 0:NG], bank[1][0:1, 0:NG], steps[0:1, 1, :], ALU.min))
            chain(dve.tensor_scalar(units[:, 0, 0:NG], units[:, 0, 0:NG], 0.0, None, ALU.max))
            chain(dve.memset(units[:, 1, 0:1], 0.0))
            chain(dve.tensor_tensor_scan(units[:, 1, 1:NG + 1], ones[0:1, 0:NG], units[:, 0, 0:NG], 0.0, ALU.add, ALU.min))
            dve.tensor_copy(plan[:, :], units[:, 1, :]).then_inc(s_plan, 1)
            dve.wait_ge(s_wts, 16 * 21)
            for l in range(2):
                dve.tensor_tensor(Wc[l][C:P, :], Wc[l][C:P, :], Wtmp[C:P, l, :], ALU.subtract).then_inc(s_wcat, 1)

            def edges(ph, unit=None):
                conv = ph in (EC1, EC2)
                fo = 0 if ph == EC1 else K

                def stage_flags(h, s):
                    need(dve, s_flT, done(ph, h, s) - 2)
                    held(dve)
                    dve.tensor_copy(fl[s][:, :], flags[:, bass.ds(group(ph, h, s), 1), fo:fo + K].rearrange("p a k -> p (a k)")).then_inc(s_fl, 1)

                def front(h, s):
                    n = done(ph, h, s)
                    stage_flags(h, s)
                    if ph == EC1:
                        rowsG = G[s][:, :, :].rearrange("p k (a c) -> p (k a) c", a=2)
                        rowsH = H[s][:, :, :].rearrange("p k (a c) -> p (k a) c", a=2)
                        dve.wait_ge(s_g[s], gath(ph, h))
                        dve.tensor_reduce(ln[s][:, 0, :], rowsG, AX, ALU.add).then_inc(s_sum, 1)
                        dve.wait_ge(s_sum, n)
                        dve.tensor_scalar(ln[s][:, 1, :], ln[s][:, 0, :], 1.0 / C, None, ALU.mult).then_inc(s_mean, 1)
                        dve.wait_ge(s_mean, n)
                        dve.tensor_tensor(xc[s][:, :, :], rowsG, ln[s][:, 1, :].unsqueeze(2).to_broadcast([P, 2 * K, C]), ALU.subtract).then_inc(s_xc, 1)
                        dve.wait_ge(s_sq, n)
                        dve.tensor_reduce(ln[s][:, 2, :], sq[s][:, :, :], AX, ALU.add).then_inc(s_ssq, 1)
                        dve.wait_ge(s_std, n)
                        dve.reciprocal(ln[s][:, 4, :], ln[s][:, 3, :]).then_inc(s_rstd, 1)
                        dve.wait_ge(s_rstd, n)
                        need(dve, s_T, n - 2)
                        dve.scalar_tensor_tensor(rowsH, xc[s][:, :, :], 0.0, ln[s][:, 4, :].unsqueeze(2).to_broadcast([P, 2 * K, C]), ALU.max, ALU.mult).then_inc(s_h, 1)
                    if ph == EC2:
                        first = isinstance(h, int) and h == 0 and s == 0
                        dve.wait_ge(s_ml[s], 16 * (h + 1))
                        dve.wait_ge(s_flT, n)
                        dve.wait_ge(s_u1, n - 2)
                        if not first:
                            dve.wait_ge(s_back, n - 1 - NG)
                        dve.tensor_tensor_scan(TS[s][C:P, ::-1], pF[s][C:P, ::-1], MF[s][C:P, ::-1],
                                               0.0 if first else TS[1 - s][C:P, 0:1], ALU.mult, ALU.max).then_inc(s_back, 1)

                def scan(h, s):
                    n = done(ph, h, s)
                    first = isinstance(h, int) and h == 0 and s == 0
                    dve.wait_ge(s_flT, n)
                    need(dve, s_mT, n - 2)
                    need(dve, s_scan, n - 1)
                    if conv:
                        need(dve, s_st, n - 2)
                        held(dve)
                        dve.tensor_copy(mk[s][:, :], masks[:, bass.ds(group(ph, h, s), 1), fo:fo + K].rearrange("p a k -> p (a k)")).then_inc(s_mk, 1)
                        dve.wait_ge(s_a2, n)
                        data = A2[s][:, :]
                    else:
                        dve.wait_ge(s_TS, n)
                        data = TS[s][0:C, :]
                    if ph == EC1 and not (isinstance(h, int) and h == 0):
                        dve.wait_ge(s_ms[s], 16 * h)
                    if ph == EC2:
                        if not first:
                            dve.wait_ge(s_cnt, n - 1 - NG)
                        dve.tensor_tensor_scan(M[s][C:CB, ::-1], pF[s][C:CB, ::-1], ones[C:CB, :],
                                               0.0 if first else M[1 - s][C:CB, 0:1], ALU.mult, ALU.add).then_inc(s_cnt, 1)
                    way, carry = (1, GE - 1) if ph == EC1 else (-1, 0)
                    same = pF[s] if conv else pFg
                    dve.tensor_tensor_scan(M[s][0:C, ::way], same[0:C, ::way], data[:, ::way],
                                           0.0 if first else M[1 - s][0:C, carry:carry + 1],
                                           ALU.mult, ALU.max if conv else ALU.add).then_inc(s_scan, 1)

                def add_stats(h, s):
                    n = done(ph, h, s)
                    dve.wait_ge(s_st, n)
                    need(dve, s_acc, n - 1)
                    dve.tensor_tensor(acc[:, :, :], acc[:, :, :], pS[s][0:1, 0:2 * C].rearrange("p (j c) -> p j c", j=2), ALU.add).then_inc(s_acc, 1)

                def conv_step(h, s):
                    front(h, s)
                    if not (isinstance(h, int) and h == 0 and s == 0):
                        scan(*((h, 0) if s == 1 else (h - 1, 1)))
                    if s == 1 and not (isinstance(h, int) and h < 1):
                        add_stats(h - 1, 0)
                    if s == 0 and not (isinstance(h, int) and h < 2):
                        add_stats(h - 2, 1)

                def gcn_step(h, s, last=False):
                    at_step = plan_at(dve, h, s)
                    if_planned(dve, at_step, unit[0])
                    scan(h, s)
                    if not last:
                        stage_flags(*((h, 1) if s == 0 else (h + 1, 0)))
                    if_planned(dve, at_step, unit[1])

                if conv:
                    run(dve, conv_step)
                else:
                    stage_flags(0, 0)
                    run(dve, gcn_step, lambda h, s: gcn_step(h, s, True))
                if conv:
                    scan(NG // 2 - 1, 1)
                    add_stats(NG // 2 - 2, 1)
                    add_stats(NG // 2 - 1, 0)
                    add_stats(NG // 2 - 1, 1)

            bn_steps = [0]

            def bn_chain(ins):
                bn_steps[0] += 1
                ins.then_inc(s_bn, 1)
                dve.wait_ge(s_bn, bn_steps[0])

            def batch_norm(ph, ga, be):
                dve.wait_ge(s_acc, NG * (ph + 1))
                b = lambda j: bn[0:C, j:j + 1]
                dve.wait_ge(s_bnc, ph + 1)
                bn_chain(dve.tensor_scalar(bn[0:C, 0:2], pS[0][0:C, 0:2], 1.0 / N, None, ALU.mult))
                bn_chain(dve.tensor_tensor(b(2), b(0), b(0), ALU.mult))
                bn_chain(dve.tensor_tensor(b(3), b(1), b(2), ALU.subtract))
                bn_chain(dve.tensor_scalar(b(3), b(3), 0.0, None, ALU.max))
                dve.wait_ge(s_bnsd, ph + 1)
                bn_chain(dve.reciprocal(b(4), b(4)))
                bn_chain(dve.tensor_tensor(b(5), b(4), cols[0:C, ga:ga + 1], ALU.mult))
                bn_chain(dve.tensor_tensor(b(6), b(0), b(5), ALU.mult))
                bn_chain(dve.tensor_tensor(b(7), cols[0:C, be:be + 1], b(6), ALU.subtract))

            edges(EC1)
            batch_norm(EC1, GA1, BE1)
            for t, j in ((a1, 5), (c1, 7)):
                bn_chain(dve.tensor_copy(t[0:C, :], bn[0:C, j:j + 1]))
                bn_chain(dve.tensor_copy(t[C:P, :], bn[0:C, j:j + 1]))
            bn_chain(dve.tensor_scalar(Weff[:, :], Wc[1][:, :], a1[:, :], None, ALU.mult))
            dve.wait_ge(s_bnp, 1)
            bn_chain(dve.tensor_tensor(bias2[:, :], pS[0][0:C, 8:9], cols[0:C, B2A:B2A + 1], ALU.add))
            bn_chain(dve.memset(acc[:, :, :], 0.0))
            dve.drain().then_inc(s_fold, 1)
            BN1_STEPS = bn_steps[0]
            edges(EC2)
            batch_norm(EC2, GA2, BE2)
            for j, c in ((0, 5), (1, 7)):
                bn_chain(dve.tensor_scalar(diag[:, j, :], ident[0:C, 0:C], bn[0:C, c:c + 1], None, ALU.mult))
            dve.wait_ge(s_bnp, 2)
            bn_chain(dve.tensor_copy(bnrow[:, :, :], pU1[:, 0:2 * C].rearrange("p (j c) -> p j c", j=2)))
            dve.drain().then_inc(s_fold, 1)

            def squares(h, s):
                dve.wait_ge(s_dsq, 2 * h + s + 1)
                dve.tensor_reduce(ln[s][:, 2, :], sq[s][:, :, :], AX, ALU.add).then_inc(s_ssq, 1)

            def factors(h, s):
                n = 2 * h + s + 1
                m = NG + n
                d = dis[:, bass.ds(2 * h + s, 1), :].rearrange("p a r -> p (a r)")
                dve.wait_ge(s_std, m)
                dve.reciprocal(ln[s][:, 4, :], ln[s][:, 3, :]).then_inc(s_rstd, 1)
                dve.wait_ge(s_rstd, m)
                dve.wait_ge(s_dis, n)
                dve.tensor_tensor(ln[s][:, 4, :], ln[s][:, 4, :], d, ALU.mult).then_inc(s_drs, 1)

            def stream(h, s):
                n = 2 * h + s + 1
                m = NG + n
                first = isinstance(h, int) and h == 0 and s == 0
                prev = (h, 0) if s == 1 else (h - 1, 1)
                d = dis[:, bass.ds(2 * h + s, 1), :].rearrange("p a r -> p (a r)")
                if not first:
                    squares(*prev)
                dve.wait_ge(s_v, 2 * n)
                if not (isinstance(h, int) and h == 0):
                    dve.wait_ge(s_x1w[s], 16 * h)
                dve.tensor_tensor(Z[s][:, :, :], U[s][:, :, :], V[s][:, :, :], ALU.add).then_inc(s_x1, 1)
                if not first:
                    factors(*prev)
                dve.wait_ge(s_x1, n)
                dve.tensor_reduce(ln[s][:, 0, :], Z[s][:, :, :], AX, ALU.add).then_inc(s_sum, 1)
                dve.wait_ge(s_deg, n)
                dve.reciprocal(d, deg[s][:, :]).then_inc(s_dis, 1)
                dve.wait_ge(s_sum, m)
                dve.tensor_scalar(ln[s][:, 1, :], ln[s][:, 0, :], 1.0 / C, None, ALU.mult).then_inc(s_mean, 1)
                dve.wait_ge(s_mean, m)
                need(dve, s_o, n - 2)
                dve.tensor_tensor(xc[s][:, :, :], Z[s][:, :, :], ln[s][:, 1, :].unsqueeze(2).to_broadcast([P, R, C]), ALU.subtract).then_inc(s_xc, 1)

            run(dve, stream)
            squares(NG // 2 - 1, 1)
            factors(NG // 2 - 1, 1)

            def dis_rows(v, j):
                return dis[:, bass.ds(node_group(v, j), 1), :].rearrange("p a r -> p (a r)").unsqueeze(2).to_broadcast([P, R, C])

            def gcn_operands(v):
                n = lambda j: 2 * v + j + 1 + s_credit
                for j in range(2):
                    dve.wait_ge(s_ld[1][j], 32 * (v + 1))
                    dve.tensor_tensor(U[j][:, :, :], DA[j][:, :, :], DC[j][:, :, :], ALU.add).then_inc(s_used, 1)
                    dve.wait_ge(s_used, n(j))
                    dve.wait_ge(s_zT, n(j) - 2)
                    held(dve)
                    dve.tensor_tensor(Z[j][:, :, :], U[j][:, :, :], dis_rows(v, j), ALU.mult).then_inc(s_z, 1)

            def gcn_results(v):
                n = lambda j: 2 * v + j + 1 + s_credit
                for j in range(2):
                    dve.wait_ge(s_gm, n(j))
                    dve.wait_ge(s_wr[1][j], 16 * (v + 1))
                    held(dve)
                    dve.tensor_tensor(O[j][:, :, :], pG[:, :].rearrange("p (r c) -> p r c", c=C), dis_rows(v, j), ALU.mult).then_inc(s_o, 1)

            def final_operands(v):
                n = lambda j: 2 * v + j + 1
                for j in range(2):
                    dve.wait_ge(s_ld[2][j], 48 * (v + 1))
                    dve.tensor_tensor(U[j][:, :, :], DA[j][:, :, :], DC[j][:, :, :], ALU.add).then_inc(s_f0, 1)
                    dve.wait_ge(s_f0, n(j))
                    held(dve)
                    dve.tensor_tensor(Z[j][:, :, :], U[j][:, :, :], dis_rows(v, j), ALU.mult).then_inc(s_f1, 1)

            def final_results(v):
                n = lambda j: 2 * v + j + 1
                for j in range(2):
                    dve.wait_ge(s_f1, n(j))
                    dve.tensor_tensor(U[j][:, :, :], Z[j][:, :, :], gb2r[:, :].unsqueeze(1).to_broadcast([P, R, C]), ALU.add).then_inc(s_f2, 1)
                    dve.wait_ge(s_f2, n(j))
                    dve.wait_ge(s_wr[2][j], 16 * (v + 1))
                    dve.scalar_tensor_tensor(O[j][:, :, :], U[j][:, :, :], 0.0, V[j][:, :, :], ALU.max, ALU.add).then_inc(s_o, 1)

            def both(first, second):
                def unit(v):
                    first(v)
                    second(v)
                return unit

            dve.sem_inc(s_used, s_credit)
            dve.sem_inc(s_z, s_credit)
            edges(GCN1, (gcn_operands, gcn_results))
            remaining(dve, both(gcn_operands, gcn_results))
            edges(GCN2, (final_operands, final_results))
            remaining(dve, both(final_operands, final_results))

        @block.tensor
        def _(pe):
            pe.wait_ge(s_rows, 1)
            for a in range(8):
                for c in range(CH):
                    last = pe.transpose(bank[a][:, c * P:(c + 1) * P], rows[:, a, c, :], ident[:, :])
            last.then_inc(s_rowsT, 1)
            pe.wait_ge(s_idx, 8)
            for c in range(CH):
                last = pe.matmul(bank[0][:, c * P:(c + 1) * P], rows[:, 8, c, P - 1:P].to_broadcast([P, P]), ident[:, :], start=True, stop=True)
            last.then_inc(s_last, 1)
            pe.wait_ge(s_ready, 1)
            pe.matmul(bank[1][0:1, 0:NG], ones[0:UNITS, 0:1], ready[0:UNITS, :], start=True, stop=True).then_inc(s_avail, 1)
            pe.wait_ge(s_plan, 1)
            def edges(ph, unit=None):
                conv = ph in (EC1, EC2)
                width = CB if ph == EC2 else C

                def front(h, s):
                    n = done(ph, h, s)
                    pe.wait_ge(s_fl, n)
                    need(pe, s_scan, n - 2 if conv else n - 1)
                    for k in range(K):
                        last = pe.matmul((pF[s] if conv else pFg)[:, k * P:(k + 1) * P], fl[s][:, k:k + 1].to_broadcast([P, P]), ident16[:, :], start=True, stop=True)
                    last.then_inc(s_flT, 1)
                    need(pe, s_TS, n - 1)
                    if ph == EC1:
                        pe.wait_ge(s_h, n)
                        for k in range(K):
                            last = pe.transpose(pT[:, k * P:(k + 1) * P], H[s][:, k, :], ident[:, :])
                        last.then_inc(s_T, 1)
                    else:
                        pe.wait_ge(s_g[s], gath(ph, h))
                        held(pe)
                        for k in range(K):
                            last = pe.transpose(pT[0:C, k * P:(k + 1) * P], G[s][:, k, 0:C], ident[:, :])
                        last.then_inc(s_T, 1)

                def turn_result(h, s):
                    n = done(ph, h, s)
                    pe.wait_ge(s_scan, n)
                    need(pe, s_mt, n - 1)
                    if conv:
                        need(pe, s_mq, n - 1)
                    held(pe)
                    for k in range(K):
                        last = pe.transpose(pBk[:, k, 0:width], M[s][0:width, k * P:(k + 1) * P], ident[0:width, 0:width])
                    last.then_inc(s_mT, 1)

                def stats(h, s):
                    n = done(ph, h, s)
                    pe.wait_ge(s_mk, n)
                    pe.wait_ge(s_mq, n)
                    need(pe, s_acc, n - 2)
                    for k in range(K):
                        last = pe.matmul(pS[s][0:1, 0:2 * C], mk[s][:, k:k + 1], MT[s][:, k, :, 0:C], start=k == 0, stop=k == K - 1)
                    last.then_inc(s_st, 1)

                def layer1(h, s):
                    n = done(ph, h, s)
                    pe.wait_ge(s_TS, n)
                    if ph == EC2:
                        pe.wait_ge(s_back, n - NG)
                    need(pe, s_a1, n - 1)
                    pe.matmul(pU1[0:C, :], (Wc[0] if ph == EC1 else Weff)[:, :], TS[s][:, :], start=True, stop=True).then_inc(s_u1, 1)

                def layer2(h, s):
                    n = done(ph, h, s)
                    pe.wait_ge(s_a1, n)
                    need(pe, s_a2, n - 1)
                    held(pe)
                    pe.matmul(pU2[0:C, :], Wb[0 if ph == EC1 else 1][:, :], A1[:, :], start=True, stop=True).then_inc(s_u2, 1)

                def step(h, s):
                    first = isinstance(h, int) and h == 0 and s == 0
                    prev = (h, 0) if s == 1 else (h - 1, 1)
                    front(h, s)
                    if conv and not first:
                        layer2(*prev)
                    if conv:
                        layer1(h, s)
                    if conv and not (isinstance(h, int) and h == 0):
                        stats(h - 1, s)
                    if not first:
                        turn_result(*prev)
                    if unit:
                        planned(pe, h, s, unit)

                run(pe, step)
                if conv:
                    layer2(NG // 2 - 1, 1)
                    stats(NG // 2 - 1, 0)
                turn_result(NG // 2 - 1, 1)
                if conv:
                    stats(NG // 2 - 1, 1)
                    pe.wait_ge(s_acc, NG * (ph + 1))
                    for j in range(2):
                        last = pe.matmul(pS[0][0:C, j:j + 1], acc[0:1, j, :], ones[0:1, 0:1], start=True, stop=True)
                    last.then_inc(s_bnc, 1)

            pe.wait_ge(s_wcat, 2)
            edges(EC1)
            pe.wait_ge(s_bn, 8 + 5)
            pe.matmul(pS[0][0:C, 8:9], Wc[1][:, :], c1[:, :], start=True, stop=True).then_inc(s_bnp, 1)
            pe.wait_ge(s_fold, 1)
            edges(EC2)
            pe.wait_ge(s_bn, 8 + 5 + 2 + 8 + 2)
            for j in range(2):
                last = pe.matmul(pU1[:, j * C:(j + 1) * C], ones[0:C, 0:P], diag[:, j, :], start=True, stop=True)
            last.then_inc(s_bnp, 1)

            def gcn_unit(v):
                n = lambda j: 2 * v + j + 1 + s_credit
                for j in range(2):
                    pe.wait_ge(s_z, n(j))
                    pe.wait_ge(s_zTS, n(j) - 2)
                    for i in range(R // 2):
                        last = pe.transpose(pZT[j][:, i * P:(i + 1) * P], Z[j][:, 2 * i:2 * i + 2, :].rearrange("p r c -> p (r c)"), ident[:, :])
                    last.then_inc(s_zT, 1)
                for j in range(2):
                    pe.wait_ge(s_zTS, n(j))
                    for half in range(2):
                        pe.wait_ge(s_hr, 2 * (n(j) - 1) - 1 + half)
                        pe.matmul(pH[half][:, :], gw1[half * C:(half + 1) * C, :], ZT[j][half * C:(half + 1) * C, :], start=True, stop=True).then_inc(s_hm, 1)
                    pe.wait_ge(s_o, ND + 2 * v + j)
                    for r in [*range(0, R, 2), *range(1, R, 2)]:
                        if r < 2:
                            pe.wait_ge(s_hr, 2 * n(j) - 1 + r)
                        last = pe.matmul(pG[:, r * C:(r + 1) * C], HT[:, r % 2, (r // 2) * P:(r // 2 + 1) * P], gw2[:, :], start=True, stop=True)
                    last.then_inc(s_gm, 1)

            pe.sem_inc(s_zT, s_credit)
            pe.sem_inc(s_hm, 2 * s_credit)
            pe.sem_inc(s_gm, s_credit)
            edges(GCN1, gcn_unit)
            remaining(pe, gcn_unit)
            edges(GCN2)


_INS = ["x", "src", "dst", "L0_gnn_W1a", "L0_gnn_b1a", "L0_gnn_W1b", "L0_gnn_b1b", "L0_gnn_gamma1", "L0_gnn_beta1",
        "L0_gnn_W2a", "L0_gnn_b2a", "L0_gnn_W2b", "L0_gnn_b2b", "L0_gnn_gamma2", "L0_gnn_beta2",
        "L1_gnn_W1", "L1_gnn_b1", "L1_gnn_W2", "L1_gnn_b2"]


def kernel(**inputs):
    import numpy as _np
    import concourse.bacc as _bacc
    from concourse import mybir as _mybir
    from concourse.bass_utils import run_bass_kernel_spmd as _run

    nc = _bacc.Bacc("TRN2", target_bir_lowering=False, num_devices=1)
    arrays, args = {}, []
    for name in _INS:
        a = _np.ascontiguousarray(inputs[name])
        arrays[f"in_{name}"] = a
        args.append(nc.dram_tensor(f"in_{name}", a.shape, _mybir.dt.from_np(a.dtype), kind="ExternalInput").ap())
    args.append(nc.dram_tensor("out_0", (N, C), F32, kind="ExternalOutput").ap())
    build(nc, *args)
    r = _run(nc, [arrays], core_ids=[0])
    return r.results[0]["out_0"]
```

```python
import concourse.bass as bass
import concourse.mybir as mybir
from concourse.alu_op_type import AluOpType as ALU
from contextlib import ExitStack


F32, BF16, I32 = mybir.dt.float32, mybir.dt.bfloat16, mybir.dt.int32
ACT = mybir.ActivationFunctionType
AX = mybir.AxisListType.X

P = 128
N, E, C, HID = 100000, 50000, 64, 128
K = 4
GE = K * P
TILES = -(-E // P)
NG = -(-TILES // (2 * K)) * 2
CH = 4
R = 8
GN = R * P
ND = -(-N // (2 * GN)) * 2
NP = ND * GN
LASTP = (N - (ND - 1) * GN) // R
CB = C + 1
PAD = float(2 ** 20)
EPS = 1e-5
ZA, ZA_FIRST, ZB = 28, 6, NG // 2
ZA_STEPS = (range(0), range(ZA_FIRST, 12), range(12, 20), range(20, ZA))
ZC = NP * C // P // ZA
assert (ND - 1) * GN < N and LASTP * R == N - (ND - 1) * GN and NG == ND
assert NP * C // P % ZA == 0 and NP // P % ZB == 0 and NP * CB // P // ZB <= ZC
assert CH * P >= NG * K and PAD > N

UNITS = (ND - 2) // 2
LAG = 4
RAW_LOADS = 3 * 3 + 5

EC1, EC2, GCN1, GCN2 = range(4)


def build(nc, x, src, dst, W1a, b1a, W1b, b1b, gamma1, beta1, W2a, b2a, W2b, b2b, gamma2, beta2,
          gW1, gb1, gW2, gb2, out):
    def dram(name, shape):
        return nc.dram_tensor(name, shape, F32, kind="Internal").ap()

    tabA = dram("tabA", (NP, C))
    tabB = dram("tabB", (NP, CB))
    m1e = dram("m1e", (NG * C, GE))
    x1 = dram("x1", (NP, C))
    hs = dram("hs", (NP, C))
    gt = dram("gt", (NP, C))

    def nodes(t, c=C):
        return t.rearrange("(g p r) c -> g p (r c)", p=P, r=R)

    m1e_g = m1e.rearrange("(g c) e -> g c e", c=C)
    tabA_g, tabB_g, x1_g, hs_g, gt_g = (nodes(t) for t in (tabA, tabB, x1, hs, gt))
    FULL = (ND - 1) * GN
    x_g, out_g = nodes(x[0:FULL, :]), nodes(out[0:FULL, :])
    x_last = x[FULL:N, :].rearrange("(p r) c -> p (r c)", r=R)
    out_last = out[FULL:N, :].rearrange("(p r) c -> p (r c)", r=R)

    with ExitStack() as ctx:
        def sb(name, shape, dt=F32):
            return ctx.enter_context(nc.sbuf_tensor(name, shape, dt))

        def sem(name):
            return ctx.enter_context(nc.semaphore(name))

        def two(name, shape, dt=F32):
            return [sb(f"{name}{s}", shape, dt) for s in range(2)]

        zeros = sb("zeros", [P, ZC])
        ident = sb("ident", [P, P])
        ident16 = sb("ident16", [P, P], BF16)
        ones = sb("ones", [P, GE])
        eps = sb("eps", [P, 1])
        raw = sb("raw", [P, 4, CH, P], I32)
        rows = sb("rows", [P, 10, CH, P])
        gidx = sb("gidx", [P, NG, 2 * K], I32)
        sidx = sb("sidx", [P, NG, 2 * K], I32)
        flags = sb("flags", [P, NG, 2 * K], BF16)
        masks = sb("masks", [P, NG, 2 * K])
        Wc = [sb(f"Wc{l}", [P, C]) for l in range(2)]
        Wtmp = sb("Wtmp", [P, 2, C])
        Weff = sb("Weff", [P, C])
        Wb = [sb(f"Wb{l}", [C, C]) for l in range(2)]
        cols = sb("cols", [P, 12])
        B1A, B1B, GA1, BE1, B2A, B2B, GA2, BE2, GB1 = range(9)
        gw1 = sb("gw1", [P, HID])
        gw2 = sb("gw2", [HID, C])
        gb2r = sb("gb2r", [P, C])
        acc = sb("acc", [1, 2, C])
        bn = sb("bn", [P, 8])
        a1, c1, bias2 = sb("a1", [P, 1]), sb("c1", [P, 1]), sb("bias2", [C, 1])
        diag = sb("diag", [C, 2, C])
        bnrow = sb("bnrow", [P, 2, C])
        gi, si = two("gi", [P, 2 * K], I32), two("si", [P, K], I32)
        fl, mk = two("fl", [P, K], BF16), two("mk", [P, K])
        G = two("G", [P, K, 2 * C])
        MF = two("MF", [P, GE])
        xc, sq = two("xc", [P, 2 * K, C]), two("sq", [P, 2 * K, C])
        H = two("H", [P, K, 2 * C])
        XC = [t[:, :, :] for t in xc] + [t[:, :, :].rearrange("p k (a c) -> p (k a) c", a=2) for t in H]
        ln = two("ln", [P, 5, R])
        TS = two("TS", [P, GE])
        A1 = sb("A1", [C, GE])
        A2 = two("A2", [C, GE])
        M = two("M", [CB, GE])
        MT = two("MT", [P, K, 2, CB])
        dis = sb("dis", [P, ND, R])
        deg = two("deg", [P, R])
        DA, DC = two("DA", [P, R, C]), two("DC", [P, R, C])
        X0 = DA + [sb(f"X{s}", [P, R, C]) for s in (2, 3)]
        DB = [sb(f"DB{s}", [P, R, CB]) for s in range(4)]
        U, V = two("U", [P, R, C]), two("V", [P, R, C])
        Z, O = two("Z", [P, R, C]), two("O", [P, R, C])
        X1 = Z + [sb(f"X1{s}", [P, R, C]) for s in (2, 3)]
        HS = O + [sb(f"HS{s}", [P, R, C]) for s in (2, 3)]
        ZT = two("ZT", [P, GE])
        HT = sb("HT", [P, 2, GE])
        iota_i = sb("iota_i", [P, 4, NG], I32)
        steps = sb("steps", [P, 4, NG])
        below = sb("below", [P, NG])
        missing = sb("missing", [P, 2])
        ready = sb("ready", [P, NG])
        units = sb("units", [1, 2, NG + 1])
        plan = sb("plan", [1, NG + 1], I32)

        bank = [ctx.enter_context(nc.psum_tensor(f"bank{b}", [P, GE], F32)) for b in range(8)]
        pT, pU1, pU2, pB, pS = bank[0], bank[3], bank[4], bank[5], [bank[6], bank[7]]
        pF = [bank[1], bank[2]]
        pBk = pB[:, 0:K * CB].rearrange("p (k c) -> p k c", c=CB)
        pFg, pZT, pH, pG = bank[1], [bank[2], bank[3]], [bank[4], bank[6]], bank[7]

        s_held = sem("held")
        s_const, s_ident, s_zero = sem("const_built"), sem("ident_ready"), sem("zero_ready")
        s_raw, s_wts, s_pad = sem("raw_loaded"), sem("weights_loaded"), sem("pad_written")
        s_zA, s_zB = sem("tabA_cleared"), sem("tabB_cleared")
        s_rows, s_rowsT, s_idx = (sem(n) for n in (
            "rows_ready", "rows_turned", "indices_ready"))
        s_iota, s_last, s_ready, s_avail, s_plan = (sem(n) for n in (
            "iota_ready", "last_dst_spread", "ready_marked", "ready_counted", "plan_ready"))
        s_wcat, s_set = sem("weights_stacked"), sem("setup_step")
        s_gi, s_si = [sem(f"gather_idx{s}") for s in range(2)], [sem(f"scatter_idx{s}") for s in range(2)]
        s_g, s_sc = [sem(f"gathered{s}") for s in range(2)], [sem(f"scattered{s}") for s in range(2)]
        s_ml, s_ms = [sem(f"m1e_loaded{s}") for s in range(2)], [sem(f"m1e_stored{s}") for s in range(2)]
        s_fl, s_mk, s_flT = sem("flags_staged"), sem("masks_staged"), sem("flags_spread")
        s_sum, s_mean, s_xc, s_sq, s_ssq, s_std, s_rstd, s_h = (sem(n) for n in (
            "ln_sum", "ln_mean", "ln_centred", "ln_squared", "ln_sumsq", "ln_std", "ln_rstd", "ln_out"))
        s_T, s_TS, s_back = sem("turned"), sem("turned_copied"), sem("dst_spread")
        s_u1, s_a1, s_u2, s_a2 = sem("layer1_sum"), sem("layer1_out"), sem("layer2_sum"), sem("layer2_out")
        s_scan, s_cnt, s_mT, s_mt, s_mq = (sem(n) for n in (
            "scanned", "counted", "result_turned", "result_copied", "result_squared"))
        s_st, s_acc = sem("stats_sum"), sem("stats_added")
        s_bnc = sem("bn_columns")
        s_bn, s_bnsd, s_bnp, s_fold = sem("bn_step"), sem("bn_std"), sem("bn_product"), sem("bn_folded")
        s_ld = [[sem(f"dense_loaded{ph}{s}") for s in range(2 if ph else 4)] for ph in range(3)]
        s_wr = [[sem(f"dense_stored{ph}{s}") for s in range(2 if ph else 4)] for ph in range(3)]
        s_x1w = [sem(f"x1_stored{s}") for s in range(4)]
        s_v, s_x1, s_used, s_o = sem("dense_shifted"), sem("stream_ready"), sem("dense_used"), sem("dense_out")
        s_deg, s_dis, s_dsq, s_drs = sem("degree_root"), sem("dis_ready"), sem("dense_squared"), sem("dense_rstd")
        s_z0, s_z, s_zT, s_zTS = sem("agg_added"), sem("agg_scaled"), sem("agg_turned"), sem("agg_copied")
        s_hm, s_hr, s_gm = sem("hidden_sum"), sem("hidden_out"), sem("gcn_product")
        s_credit = 2
        s_f0, s_f1, s_f2 = sem("final_added"), sem("final_scaled"), sem("final_biased")

        def need(eng, s, value):
            if not (isinstance(value, int) and value <= 0):
                eng.wait_ge(s, value)

        def held(eng):
            eng.sem_inc(s_held, 1)

        def run(eng, step, last=None):
            for h in range(2):
                step(h, 0)
                step(h, 1)
            if last is None:
                with eng.Fori(2, NG // 2) as h:
                    step(h, 0)
                    step(h, 1)
            else:
                with eng.Fori(2, NG // 2 - 1) as h:
                    step(h, 0)
                    step(h, 1)
                step(NG // 2 - 1, 0)
                last(NG // 2 - 1, 1)

        def run_dense(eng, step):
            for h in range(2):
                for s in range(2):
                    step(h, s, 2 * h + s, 1)
            with eng.Fori(1, NG // 4) as q:
                for j in range(4):
                    step(2 * q + j // 2, j % 2, j, q + 1)
            for s in range(2):
                step(NG // 2 - 1, s, s, NG // 4 + 1)

        def done(ph, h, s):
            return NG * ph + 2 * h + s + 1

        def gath(ph, h):
            before = 0 if ph == EC1 else 16 * K * (NG // 2) * (ph + 1)
            return before + 16 * K * (2 if ph == EC1 else 1) * (h + 1)

        def scat(ph, h):
            return 16 * K * ((NG // 2) * ph + h + 1)

        wA = NP * C // P // ZA
        vA = tabA.rearrange("(z p r) c -> z p (r c)", z=ZA, p=P)

        def at(t, h, s):
            return t[bass.ds(2 * h + s, 1), :, :].rearrange("a p f -> p (a f)")

        def flat(t):
            return t[:, :, :].rearrange("p r c -> p (r c)")

        def node_io(h, s, last, tile, whole, part):
            if last:
                return flat(tile)[0:LASTP, :], part
            return flat(tile), at(whole, h, s)

        def group(ph, h, s):
            return 2 * h + s if ph == EC1 else (NG - 1 - s) - 2 * h

        def node_group(v, j):
            if isinstance(v, int) and v == UNITS:
                return 0 if j else ND - 1
            return (ND - 2 - j) - 2 * v

        def rows_of(t, g):
            return t[bass.ds(g, 1), :, :].rearrange("a p f -> p (a f)")

        def plan_at(eng, h):
            if isinstance(h, int) and 2 * h + 1 < LAG:
                return None
            before = eng.value_load(plan[0:1, bass.ds(2 * h + 1, 1)], min_val=0, max_val=UNITS - 1)
            after = eng.value_load(plan[0:1, bass.ds(2 * h + 2, 1)], min_val=0, max_val=UNITS)
            return before, after

        def planned(eng, plan_of_pair, *parts):
            if plan_of_pair is not None:
                before, after = plan_of_pair
                with eng.If(after > before):
                    for part in parts:
                        part(before)

        def run_pairs(eng, pair):
            pair(0)
            pair(1)
            with eng.Fori(2, NG // 2 - 1) as h:
                pair(h)
            pair(NG // 2 - 1)

        def remaining(eng, unit):
            first = eng.value_load(plan[0:1, NG:NG + 1], min_val=0, max_val=UNITS)
            with eng.If(first < UNITS):
                with eng.Fori(first, UNITS) as v:
                    unit(v)
            unit(UNITS)

        block = ctx.enter_context(nc.Block())

        @block.sync
        def _(sp):
            sp.wait_ge(s_pad, 1)
            W = P * (CH - 1)
            T6 = E // P - W
            rest = E - (E // P) * P

            def load_rows(a, v, shift):
                last = rest - max(shift, 0)
                if shift >= 0:
                    full = v[shift:shift + W * P].rearrange("(c t e) -> t c e", t=P, e=P)
                    sp.dma_start(raw[:, a, 0:CH - 1, :], full).then_inc(s_raw, 16)
                else:
                    sp.dma_start(raw[0:1, a, 0, 1:P], v[0:P - 1].rearrange("(t e) -> t e", t=1)).then_inc(s_raw, 16)
                    sp.dma_start(raw[1:P, a, 0, :], v[P - 1:P - 1 + (P - 1) * P].rearrange("(t e) -> t e", e=P)).then_inc(s_raw, 16)
                    sp.dma_start(raw[:, a, 1:CH - 1, :], v[P * P - 1:W * P - 1].rearrange("(c t e) -> t c e", t=P, e=P)).then_inc(s_raw, 16)
                b = W * P + shift
                sp.dma_start(raw[0:T6, a, CH - 1, :], v[b:b + T6 * P].rearrange("(t e) -> t e", e=P)).then_inc(s_raw, 16)
                b += T6 * P
                sp.dma_start(raw[T6:T6 + 1, a, CH - 1, 0:last], v[b:b + last].rearrange("(t e) -> t e", t=1)).then_inc(s_raw, 16)

            load_rows(0, src, 0)
            load_rows(1, dst, 0)
            load_rows(2, dst, 1)
            load_rows(3, dst, -1)
            sp.wait_ge(s_idx, 8)

            def stage(ph, h, s, back):
                need(sp, s_g[s], gath(ph, h - 1) if not (isinstance(h, int) and h == 0 and ph == EC1) else 0)
                held(sp)
                n = 2 * K if ph == EC1 else K
                sp.dma_start(gi[s][:, 0:n], gidx[:, bass.ds(group(ph, h, s), 1), 0:n].rearrange("p a n -> p (a n)")).then_inc(s_gi[s], 16)

            def stage_scatter(ph, h, s):
                need(sp, s_sc[s], scat(ph, h - 1))
                held(sp)
                o = 0 if ph == EC1 else K
                sp.dma_start(si[s][:, :], sidx[:, bass.ds(group(ph, h, s), 1), o:o + K].rearrange("p a n -> p (a n)")).then_inc(s_si[s], 16)

            def edge_loads(ph, unit=None):
                def step(h, s):
                    stage(ph, h, s, 0)
                    if ph == EC1 and isinstance(h, int):
                        for z in ZA_STEPS[2 * h + s]:
                            sp.dma_start(vA[z], zeros[:, 0:wA]).then_inc(s_zA, 16)
                    if ph == EC1 and s == 1:
                        sp.dma_start(vB[bass.ds(h, 1), :, :].rearrange("a p f -> p (a f)"), zeros[:, 0:NP * CB // P // ZB]).then_inc(s_zB, 16)
                    if ph == EC2:
                        need(sp, s_back, done(ph, h, s) - 2 - NG)
                        sp.dma_start(MF[s][C:P, :], m1e_g[bass.ds(group(ph, h, s), 1), :, :].rearrange("a c e -> c (a e)")).then_inc(s_ml[s], 16)
                    if not (isinstance(h, int) and h == 0):
                        tail(ph, h - 1, s)
                    if ph == EC1 and isinstance(h, int) and (h, s) == (0, 1):
                        load_weights()
                    if unit and s == 1:
                        planned(sp, plan_at(sp, h), unit)

                def tail(ph, h, s):
                    stage_scatter(ph, h, s)
                    if ph == EC1:
                        sp.wait_ge(s_scan, done(ph, h, s))
                        sp.dma_start(m1e_g[bass.ds(group(ph, h, s), 1), :, :].rearrange("a c e -> c (a e)"), M[s][0:C, :]).then_inc(s_ms[s], 16)

                run(sp, step)
                tail(ph, NG // 2 - 1, 0)
                tail(ph, NG // 2 - 1, 1)

            def load_weights():
                for l, (wa, wb) in enumerate(((W1a, W1b), (W2a, W2b))):
                    sp.dma_start(Wc[l][0:C, :], wa[C:2 * C, :]).then_inc(s_wts, 16)
                    sp.dma_start(Wc[l][C:P, :], wa[0:C, :]).then_inc(s_wts, 16)
                    sp.dma_start(Wtmp[C:P, l, :], wa[C:2 * C, :]).then_inc(s_wts, 16)
                    sp.dma_start(Wb[l][:, :], wb[:, :]).then_inc(s_wts, 16)
                for j, v in ((B1A, b1a), (B1B, b1b), (GA1, gamma1), (BE1, beta1), (B2A, b2a), (B2B, b2b),
                             (GA2, gamma2), (BE2, beta2), (GB1, gb1)):
                    sp.dma_start(cols[0:v.shape[0], j:j + 1], v.rearrange("(p a) -> p a", a=1)).then_inc(s_wts, 16)
                sp.dma_start(gw1[0:C, :], gW1[:, :]).then_inc(s_wts, 16)
                sp.dma_start(gw1[C:P, :], gW1[:, :]).then_inc(s_wts, 16)
                sp.dma_start(gw2[:, :], gW2[:, :]).then_inc(s_wts, 16)
                sp.dma_start(gb2r[:, :], gb2.rearrange("(a c) -> a c", a=1).to_broadcast([P, C])).then_inc(s_wts, 16)

            sp.wait_ge(s_zero, 1)
            vB = tabB.rearrange("(z p r) c -> z p (r c)", z=ZB, p=P)
            edge_loads(EC1)
            for s in range(2):
                sp.wait_ge(s_ms[s], 16 * (NG // 2))
            edge_loads(EC2)
            for s in range(2):
                sp.wait_ge(s_sc[s], scat(EC2, NG // 2 - 1))

            def stream_loads(h, s, slot, rounds):
                first = isinstance(h, int) and h < 2
                if not first:
                    sp.wait_ge(s_v, 2 * (2 * h + s - 3))
                    sp.wait_ge(s_deg, 2 * h + s - 3)
                last = isinstance(h, int) and h == NG // 2 - 1 and s == 1
                tile, rows = node_io(h, s, last, X0[slot], x_g, x_last)
                sp.dma_start(tile, rows).then_inc(s_ld[0][slot], 16)
                sp.dma_start(flat(DB[slot]), at(tabB_g, h, s)).then_inc(s_ld[0][slot], 16)
                if not first:
                    stores(h - 2, s, slot)

            def stores(h, s, slot):
                sp.wait_ge(s_x1, 2 * h + s + 1)
                sp.dma_start(at(x1_g, h, s), flat(X1[slot])).then_inc(s_x1w[slot], 16)
                sp.wait_ge(s_o, 2 * h + s + 1)
                sp.dma_start(at(hs_g, h, s), flat(HS[slot])).then_inc(s_wr[0][slot], 16)

            run_dense(sp, stream_loads)
            for s in range(2):
                stores(NG // 2 - 2, s, 2 + s)
            for s in range(2):
                stores(NG // 2 - 1, s, s)

            def gcn_loads(v):
                for j in range(2):
                    sp.wait_ge(s_used, 2 * v + j - 1 + s_credit)
                    held(sp)
                    for t, d in ((DA, hs_g), (DC, tabA_g)):
                        sp.dma_start(flat(t[j]), rows_of(d, node_group(v, j))).then_inc(s_ld[1][j], 16)

            def final_loads(v):
                for j in range(2):
                    sp.wait_ge(s_o, 2 * ND + 2 * v + j - 1)
                    held(sp)
                    for t, d in ((DA, gt_g), (DC, tabA_g), (V, x1_g)):
                        sp.dma_start(flat(t[j]), rows_of(d, node_group(v, j))).then_inc(s_ld[2][j], 16)

            sp.wait_ge(s_plan, 1)
            edge_loads(GCN1, gcn_loads)
            for s in range(2):
                sp.wait_ge(s_sc[s], scat(GCN1, NG // 2 - 1))
            remaining(sp, gcn_loads)
            for s in range(4):
                sp.wait_ge(s_x1w[s], 16 * len(range(s, NG, 4)))
            for s in range(2):
                sp.wait_ge(s_wr[1][s], 16 * (UNITS + 2))
            edge_loads(GCN2, final_loads)
            for s in range(2):
                sp.wait_ge(s_sc[s], scat(GCN2, NG // 2 - 1))
            remaining(sp, final_loads)
            for s in range(2):
                sp.wait_ge(s_wr[2][s], 16 * (UNITS + 2))

        @block.gpsimd
        def _(pool):
            pool.iota(iota_i[:, 0, :], pattern=[[1, NG]], base=0, channel_multiplier=0).then_inc(s_iota, 1)
            pool.iota(iota_i[:, 1, :].rearrange("p (h s) -> p h s", s=2), pattern=[[1, NG // 2], [1, 2]], base=-1, channel_multiplier=0).then_inc(s_iota, 1)
            pool.iota(iota_i[:, 2, :], pattern=[[0, NG]], base=(ND - 3) * GN, channel_multiplier=-2 * GN).then_inc(s_iota, 1)
            pool.iota(iota_i[:, 3, :].rearrange("p (h s) -> p h s", s=2), pattern=[[0, NG // 2], [1, 2]], base=0, channel_multiplier=0).then_inc(s_iota, 1)
            pool.memset(ident[:, :], 0.0).then_inc(s_const, 1)
            pool.wait_ge(s_const, 1)
            pool.affine_select(out=ident[:, :], in_=ident[:, :], compare_op=ALU.not_equal, fill=1.0,
                               base=0, pattern=[[-1, P]], channel_multiplier=1).then_inc(s_ident, 1)

            def edges(ph):
                table = {EC1: x, EC2: tabA, GCN1: hs, GCN2: gt}[ph]
                target = tabB if ph == EC2 else tabA
                width = CB if ph == EC2 else C

                def gather(h, s):
                    pool.wait_ge(s_gi[s], 16 * ((NG // 2) * ph + h + 1))
                    need(pool, s_xc if ph == EC1 else s_T, done(ph, h, s) - 2)
                    held(pool)
                    for k in range(K):
                        for side in range(2 if ph == EC1 else 1):
                            pool.indirect_dma_start(
                                out=G[s][:, k, side * C:(side + 1) * C], out_offset=None, in_=table[:, :],
                                in_offset=bass.IndirectOffsetOnAxis(ap=gi[s][:, side * K + k:side * K + k + 1], axis=0),
                            ).then_inc(s_g[s], 16)

                def scatter(h, s):
                    pool.wait_ge(s_si[s], 16 * ((NG // 2) * ph + h + 1))
                    pool.wait_ge(s_mt, done(ph, h, s))
                    held(pool)
                    for k in range(K):
                        pool.indirect_dma_start(
                            out=target[:, :], out_offset=bass.IndirectOffsetOnAxis(ap=si[s][:, k:k + 1], axis=0),
                            in_=MT[s][:, k, 0, 0:width], in_offset=None, bounds_check=N - 1, oob_is_err=False,
                        ).then_inc(s_sc[s], 16)

                def step(h, s):
                    gather(h, s)
                    if not (isinstance(h, int) and h == 0):
                        scatter(h - 1, s)

                if ph == EC1:
                    for h, s in ((0, 0), (0, 1), (1, 0), (1, 1), (2, 0)):
                        gather(h, s)
                    pool.wait_ge(s_zA, 16 * ZA)
                    for s in range(2):
                        scatter(0, s)
                    scatter(1, 0)
                    gather(2, 1)
                    scatter(1, 1)
                    with pool.Fori(3, NG // 2) as h:
                        step(h, 0)
                        step(h, 1)
                else:
                    run(pool, step)
                scatter(NG // 2 - 1, 0)
                scatter(NG // 2 - 1, 1)
                for s in range(2):
                    pool.wait_ge(s_sc[s], scat(ph, NG // 2 - 1))

            edges(EC1)
            pool.wait_ge(s_zB, 16 * ZB)
            edges(EC2)

            pool.wait_ge(s_fold, 2)

            def shift(h, s, slot, rounds):
                pool.wait_ge(s_ld[0][slot], 32 * rounds)
                need(pool, s_x1, done(0, h, s) - 2)
                pool.tensor_tensor(U[s][:, :, :], DB[slot][:, :, 0:C], bnrow[:, 0:1, :].to_broadcast([P, R, C]), ALU.mult).then_inc(s_v, 1)
                pool.tensor_tensor(V[s][:, :, :], X0[slot][:, :, :], bnrow[:, 1:2, :].to_broadcast([P, R, C]), ALU.add).then_inc(s_v, 1)

            run_dense(pool, shift)
            for s in range(4):
                pool.wait_ge(s_wr[0][s], 16 * len(range(s, NG, 4)))
            edges(GCN1)
            for s in range(2):
                pool.wait_ge(s_wr[1][s], 16 * (UNITS + 2))
            edges(GCN2)

        @block.scalar
        def _(act):
            def edges(ph, first_half=(), second_half=(), after_pair=()):
                conv = ph in (EC1, EC2)
                width = CB if ph == EC2 else C

                def front(h, s):
                    n = done(ph, h, s)
                    if ph == EC1:
                        act.wait_ge(s_xc, n)
                        need(act, s_ssq, n - 2)
                        act.activation(sq[s][:, :, :], xc[s][:, :, :], ACT.Square).then_inc(s_sq, 1)
                        act.wait_ge(s_ssq, n)
                        act.activation(ln[s][:, 3, :], ln[s][:, 2, :], ACT.Sqrt, bias=eps[:, :], scale=1.0 / C).then_inc(s_std, 1)
                    act.wait_ge(s_T, n)
                    if conv:
                        need(act, s_u1, n - 2)
                    else:
                        need(act, s_scan, n - 2)
                    p = P if ph == EC1 else C
                    act.activation(TS[s][0:p, :], pT[0:p, :], ACT.Copy).then_inc(s_TS, 1)

                def result(h, s):
                    n = done(ph, h, s)
                    act.wait_ge(s_mT, n)
                    need(act, s_sc[s], scat(ph, h - 1))
                    if conv:
                        need(act, s_st, n - 2)
                    act.activation(MT[s][:, :, 0, 0:width], pBk[:, :, 0:width], ACT.Copy).then_inc(s_mt, 1)
                    if conv:
                        act.activation(MT[s][:, :, 1, 0:C], pBk[:, :, 0:C], ACT.Square).then_inc(s_mq, 1)

                def layer1(h, s):
                    n = done(ph, h, s)
                    act.wait_ge(s_u1, n)
                    need(act, s_u2, n - 1)
                    act.activation(A1[:, :], pU1[0:C, :], ACT.Relu,
                                   bias=cols[0:C, B1A:B1A + 1] if ph == EC1 else bias2[:, :]).then_inc(s_a1, 1)

                def layer2(h, s):
                    n = done(ph, h, s)
                    act.wait_ge(s_u2, n)
                    need(act, s_scan, n - 2)
                    b = B1B if ph == EC1 else B2B
                    act.activation(A2[s][:, :], pU2[0:C, :], ACT.Relu, bias=cols[0:C, b:b + 1]).then_inc(s_a2, 1)

                def step(h, s):
                    first = isinstance(h, int) and h == 0 and s == 0
                    prev = (h, 0) if s == 1 else (h - 1, 1)
                    front(h, s)
                    if conv and not first:
                        layer2(*prev)
                    if conv:
                        layer1(h, s)
                    if not first:
                        result(*prev)

                def gcn_pair(h):
                    step(h, 0)
                    this = plan_at(act, h) if first_half else None
                    planned(act, this, *first_half)
                    previous = None if isinstance(h, int) and h == 0 else plan_at(act, h - 1)
                    planned(act, previous, *after_pair)
                    step(h, 1)
                    planned(act, this, *second_half)

                if conv:
                    run(act, step)
                    layer2(NG // 2 - 1, 1)
                else:
                    run_pairs(act, gcn_pair)
                result(NG // 2 - 1, 1)
                if not conv:
                    planned(act, plan_at(act, NG // 2 - 1), *after_pair)

            act.wait_ge(s_zero, 1)
            act.wait_ge(s_raw, 16 * RAW_LOADS)
            for z in range(ZA_FIRST):
                act.dma_start(vA[z], zeros[:, 0:wA]).then_inc(s_zA, 16)
            act.wait_ge(s_wts, 16 * 21)
            def deviation(steps):
                act.wait_ge(s_bn, steps)
                act.activation(bn[0:C, 4:5], bn[0:C, 3:4], ACT.Sqrt, bias=eps[0:C, :]).then_inc(s_bnsd, 1)

            edges(EC1)
            deviation(4)
            act.wait_ge(s_fold, 1)
            edges(EC2)
            deviation(8 + 5 + 2 + 4)

            def prev_of(h, s):
                return (h, 0) if s == 1 else (h - 1, 1)

            def prev_slot(slot, rounds):
                return (slot - 1, rounds) if slot else (3, rounds - 1)

            def deviation_rows(h, s):
                act.wait_ge(s_ssq, NG + 2 * h + s + 1)
                act.activation(ln[s][:, 3, :], ln[s][:, 2, :], ACT.Sqrt, bias=eps[:, :], scale=1.0 / C).then_inc(s_std, 1)

            def normal_rows(h, s, slot, rounds):
                act.wait_ge(s_drs, 2 * h + s + 1)
                if not (isinstance(h, int) and h < 2):
                    act.wait_ge(s_wr[0][slot], 16 * (rounds - 1))
                for r in range(R):
                    last = act.activation(HS[slot][:, r, :], XC[slot][:, r, :], ACT.Relu, scale=ln[s][:, 4, r:r + 1])
                last.then_inc(s_o, 1)

            def stream(h, s, slot, rounds):
                n = 2 * h + s + 1
                first = isinstance(h, int) and h == 0 and s == 0
                act.wait_ge(s_ld[0][slot], 32 * rounds)
                need(act, s_dis, n - 2)
                act.activation(deg[s][:, :], DB[slot][:, :, C:CB].rearrange("p r c -> p (r c)"), ACT.Sqrt, bias=ones[:, 0:1]).then_inc(s_deg, 1)
                if not first:
                    deviation_rows(*prev_of(h, s))
                act.wait_ge(s_xc, NG + n)
                act.activation(sq[s][:, :, :], XC[slot], ACT.Square).then_inc(s_dsq, 1)
                if not first:
                    normal_rows(*prev_of(h, s), *prev_slot(slot, rounds))

            run_dense(act, stream)
            deviation_rows(NG // 2 - 1, 1)
            normal_rows(NG // 2 - 1, 1, 1, NG // 4 + 1)

            count = lambda v, j: 2 * v + j + 1 + s_credit

            def copy_turned(v):
                for j in range(2):
                    act.wait_ge(s_zT, count(v, j))
                    act.wait_ge(s_hm, 2 * (count(v, j) - 2))
                    act.activation(ZT[j][:, :], pZT[j][:, :], ACT.Copy).then_inc(s_zTS, 1)

            def hidden(j):
                def part(v):
                    act.wait_ge(s_gm, count(v, j) - 1)
                    for half in range(2):
                        act.wait_ge(s_hm, 2 * count(v, j) - 1 + half)
                        act.activation(HT[:, half, :], pH[half][:, :], ACT.Relu, bias=cols[:, GB1:GB1 + 1]).then_inc(s_hr, 1)
                return part

            def store_gt(j):
                def part(v):
                    act.wait_ge(s_o, ND + 2 * v + j + 1)
                    act.dma_start(rows_of(gt_g, node_group(v, j)), flat(O[j])).then_inc(s_wr[1][j], 16)
                return part

            def gcn_unit(v):
                for part in (copy_turned, hidden(0), hidden(1), store_gt(0), store_gt(1)):
                    part(v)

            def store_output(v):
                for j in range(2):
                    act.wait_ge(s_o, 2 * ND + 2 * v + j + 1)
                    if isinstance(v, int) and j == 0:
                        act.dma_start(out_last, flat(O[j])[0:LASTP, :]).then_inc(s_wr[2][j], 16)
                    else:
                        act.dma_start(rows_of(out_g, node_group(v, j)), flat(O[j])).then_inc(s_wr[2][j], 16)

            act.sem_inc(s_zTS, s_credit)
            act.sem_inc(s_hr, 2 * s_credit)
            for s in range(2):
                act.sem_inc(s_wr[1][s], 16)
                act.sem_inc(s_wr[2][s], 16)
            act.wait_ge(s_plan, 1)
            edges(GCN1, (copy_turned, hidden(0)), (hidden(1), store_gt(0)), (store_gt(1),))
            remaining(act, gcn_unit)
            edges(GCN2, after_pair=(store_output,))
            remaining(act, store_output)

        @block.vector
        def _(dve):
            dve.memset(raw[:, 0, :, :], 0)
            dve.memset(raw[:, 1:4, :, :], int(PAD)).then_inc(s_pad, 1)
            dve.memset(zeros[:, :], 0.0).then_inc(s_zero, 1)
            done_set = [0]

            def chain(ins):
                done_set[0] += 1
                ins.then_inc(s_set, 1)
                dve.wait_ge(s_set, done_set[0])

            chain(dve.memset(ones[:, :], 1.0))
            chain(dve.memset(eps[:, :], EPS))
            chain(dve.memset(acc[:, :, :], 0.0))
            dve.wait_ge(s_ident, 1)
            chain(dve.tensor_copy(ident16[:, :], ident[:, :]))
            dve.wait_ge(s_raw, 16 * RAW_LOADS)
            SRC, DST, SE, SS, EQP, EQN, ME, MS, CUR, TMP = range(10)
            dve.tensor_copy(rows[:, SRC, :, :], raw[:, 0, :, :])
            chain(dve.tensor_copy(rows[:, CUR, :, :], raw[:, 1, :, :]))
            chain(dve.tensor_copy(rows[:, TMP, :, :], raw[:, 3, :, :]))
            chain(dve.tensor_tensor(rows[:, EQP, :, :], rows[:, CUR, :, :], rows[:, TMP, :, :], ALU.is_equal))
            chain(dve.tensor_copy(rows[:, TMP, :, :], raw[:, 2, :, :]))
            chain(dve.tensor_tensor(rows[:, EQN, :, :], rows[:, CUR, :, :], rows[:, TMP, :, :], ALU.is_equal))
            dve.tensor_scalar(rows[:, DST, :, :], rows[:, CUR, :, :], float(N - 1), None, ALU.min)
            dve.scalar_tensor_tensor(rows[:, SS, :, :], rows[:, EQP, :, :], PAD, rows[:, CUR, :, :], ALU.mult, ALU.add)
            chain(dve.scalar_tensor_tensor(rows[:, SE, :, :], rows[:, EQN, :, :], PAD, rows[:, CUR, :, :], ALU.mult, ALU.add))
            dve.tensor_scalar(rows[:, ME, :, :], rows[:, SE, :, :], float(N), None, ALU.is_lt)
            dve.tensor_scalar(rows[:, MS, :, :], rows[:, SS, :, :], float(N), None, ALU.is_lt).then_inc(s_rows, 1)
            dve.wait_ge(s_rowsT, 1)
            turned = ((gidx, 0, SRC), (gidx, K, DST), (sidx, 0, SE), (sidx, K, SS),
                      (flags, 0, EQP), (flags, K, EQN), (masks, 0, ME), (masks, K, MS))
            for t, o, a in turned:
                dve.tensor_copy(t[:, :, o:o + K], bank[a][:, 0:NG * K].rearrange("p (g k) -> p g k", k=K)).then_inc(s_idx, 1)
            dve.wait_ge(s_idx, len(turned))
            dve.wait_ge(s_iota, 4)
            chain(dve.tensor_copy(steps[:, :, :], iota_i[:, :, :]))
            dve.wait_ge(s_last, 1)
            chain(dve.tensor_scalar(below[:, :], bank[0][:, K - 1:NG * K:K], steps[:, 2, 0:1], None, ALU.is_lt))
            chain(dve.tensor_reduce(missing[:, 0:1], below[:, :], AX, ALU.add))
            chain(dve.tensor_scalar(missing[:, 1:2], missing[:, 0:1], -1.0, float(NG - 1 + LAG), ALU.mult, ALU.add))
            dve.tensor_scalar(ready[:, :], steps[:, 0, :], missing[:, 1:2], None, ALU.is_ge).then_inc(s_ready, 1)
            dve.wait_ge(s_avail, 1)
            chain(dve.tensor_tensor(units[:, 0, 0:NG], bank[1][0:1, 0:NG], steps[0:1, 1, :], ALU.min))
            chain(dve.tensor_scalar(units[:, 0, 0:NG], units[:, 0, 0:NG], 0.0, None, ALU.max))
            chain(dve.memset(units[:, 1, 0:1], 0.0))
            chain(dve.tensor_tensor_scan(units[:, 1, 1:NG + 1], steps[0:1, 3, :], units[:, 0, 0:NG], 0.0, ALU.add, ALU.min))
            dve.tensor_copy(plan[:, :], units[:, 1, :]).then_inc(s_plan, 1)
            dve.wait_ge(s_wts, 16 * 21)
            for l in range(2):
                dve.tensor_tensor(Wc[l][C:P, :], Wc[l][C:P, :], Wtmp[C:P, l, :], ALU.subtract).then_inc(s_wcat, 1)

            def edges(ph, this_mid=(), this_end=(), next_pair=()):
                conv = ph in (EC1, EC2)
                fo = 0 if ph == EC1 else K

                def stage_flags(h, s):
                    need(dve, s_flT, done(ph, h, s) - 2)
                    held(dve)
                    dve.tensor_copy(fl[s][:, :], flags[:, bass.ds(group(ph, h, s), 1), fo:fo + K].rearrange("p a k -> p (a k)")).then_inc(s_fl, 1)

                def front(h, s):
                    n = done(ph, h, s)
                    stage_flags(h, s)
                    if ph == EC1:
                        rowsG = G[s][:, :, :].rearrange("p k (a c) -> p (k a) c", a=2)
                        rowsH = H[s][:, :, :].rearrange("p k (a c) -> p (k a) c", a=2)
                        dve.wait_ge(s_g[s], gath(ph, h))
                        dve.tensor_reduce(ln[s][:, 0, :], rowsG, AX, ALU.add).then_inc(s_sum, 1)
                        dve.wait_ge(s_sum, n)
                        dve.tensor_scalar(ln[s][:, 1, :], ln[s][:, 0, :], 1.0 / C, None, ALU.mult).then_inc(s_mean, 1)
                        dve.wait_ge(s_mean, n)
                        dve.tensor_tensor(xc[s][:, :, :], rowsG, ln[s][:, 1, :].unsqueeze(2).to_broadcast([P, 2 * K, C]), ALU.subtract).then_inc(s_xc, 1)
                        dve.wait_ge(s_sq, n)
                        dve.tensor_reduce(ln[s][:, 2, :], sq[s][:, :, :], AX, ALU.add).then_inc(s_ssq, 1)
                        dve.wait_ge(s_std, n)
                        dve.reciprocal(ln[s][:, 4, :], ln[s][:, 3, :]).then_inc(s_rstd, 1)
                        dve.wait_ge(s_rstd, n)
                        need(dve, s_T, n - 2)
                        dve.scalar_tensor_tensor(rowsH, xc[s][:, :, :], 0.0, ln[s][:, 4, :].unsqueeze(2).to_broadcast([P, 2 * K, C]), ALU.max, ALU.mult).then_inc(s_h, 1)
                    if ph == EC2:
                        first = isinstance(h, int) and h == 0 and s == 0
                        dve.wait_ge(s_ml[s], 16 * (h + 1))
                        dve.wait_ge(s_flT, n)
                        dve.wait_ge(s_u1, n - 2)
                        if not first:
                            dve.wait_ge(s_back, n - 1 - NG)
                        dve.tensor_tensor_scan(TS[s][C:P, ::-1], pF[s][C:P, ::-1], MF[s][C:P, ::-1],
                                               0.0 if first else TS[1 - s][C:P, 0:1], ALU.mult, ALU.max).then_inc(s_back, 1)

                def scan(h, s):
                    n = done(ph, h, s)
                    first = isinstance(h, int) and h == 0 and s == 0
                    dve.wait_ge(s_flT, n)
                    need(dve, s_mT, n - 2)
                    need(dve, s_scan, n - 1)
                    if conv:
                        need(dve, s_st, n - 2)
                        held(dve)
                        dve.tensor_copy(mk[s][:, :], masks[:, bass.ds(group(ph, h, s), 1), fo:fo + K].rearrange("p a k -> p (a k)")).then_inc(s_mk, 1)
                        dve.wait_ge(s_a2, n)
                        data = A2[s][:, :]
                    else:
                        dve.wait_ge(s_TS, n)
                        data = TS[s][0:C, :]
                    if ph == EC1 and not (isinstance(h, int) and h == 0):
                        dve.wait_ge(s_ms[s], 16 * h)
                    if ph == EC2:
                        if not first:
                            dve.wait_ge(s_cnt, n - 1 - NG)
                        dve.tensor_tensor_scan(M[s][C:CB, ::-1], pF[s][C:CB, ::-1], ones[C:CB, :],
                                               0.0 if first else M[1 - s][C:CB, 0:1], ALU.mult, ALU.add).then_inc(s_cnt, 1)
                    way, carry = (1, GE - 1) if ph == EC1 else (-1, 0)
                    same = pF[s] if conv else pFg
                    dve.tensor_tensor_scan(M[s][0:C, ::way], same[0:C, ::way], data[:, ::way],
                                           0.0 if first else M[1 - s][0:C, carry:carry + 1],
                                           ALU.mult, ALU.max if conv else ALU.add).then_inc(s_scan, 1)

                def add_stats(h, s):
                    n = done(ph, h, s)
                    dve.wait_ge(s_st, n)
                    need(dve, s_acc, n - 1)
                    dve.tensor_tensor(acc[:, :, :], acc[:, :, :], pS[s][0:1, 0:2 * C].rearrange("p (j c) -> p j c", j=2), ALU.add).then_inc(s_acc, 1)

                def conv_step(h, s):
                    front(h, s)
                    if not (isinstance(h, int) and h == 0 and s == 0):
                        scan(*((h, 0) if s == 1 else (h - 1, 1)))
                    if s == 1 and not (isinstance(h, int) and h < 1):
                        add_stats(h - 1, 0)
                    if s == 0 and not (isinstance(h, int) and h < 2):
                        add_stats(h - 2, 1)

                def gcn_pair(h):
                    last = isinstance(h, int) and h == NG // 2 - 1
                    this = plan_at(dve, h)
                    following = plan_at(dve, h + 1) if next_pair and not last else None
                    stage_flags(h, 1)
                    scan(h, 0)
                    planned(dve, this, *this_mid)
                    if not last:
                        stage_flags(h + 1, 0)
                    scan(h, 1)
                    planned(dve, following, *next_pair)
                    planned(dve, this, *this_end)

                if conv:
                    run(dve, conv_step)
                else:
                    stage_flags(0, 0)
                    run_pairs(dve, gcn_pair)
                if conv:
                    scan(NG // 2 - 1, 1)
                    add_stats(NG // 2 - 2, 1)
                    add_stats(NG // 2 - 1, 0)
                    add_stats(NG // 2 - 1, 1)

            bn_steps = [0]

            def bn_chain(ins):
                bn_steps[0] += 1
                ins.then_inc(s_bn, 1)
                dve.wait_ge(s_bn, bn_steps[0])

            def batch_norm(ph, ga, be):
                dve.wait_ge(s_acc, NG * (ph + 1))
                b = lambda j: bn[0:C, j:j + 1]
                dve.wait_ge(s_bnc, ph + 1)
                bn_chain(dve.tensor_scalar(bn[0:C, 0:2], pS[0][0:C, 0:2], 1.0 / N, None, ALU.mult))
                bn_chain(dve.tensor_tensor(b(2), b(0), b(0), ALU.mult))
                bn_chain(dve.tensor_tensor(b(3), b(1), b(2), ALU.subtract))
                bn_chain(dve.tensor_scalar(b(3), b(3), 0.0, None, ALU.max))
                dve.wait_ge(s_bnsd, ph + 1)
                bn_chain(dve.reciprocal(b(4), b(4)))
                bn_chain(dve.tensor_tensor(b(5), b(4), cols[0:C, ga:ga + 1], ALU.mult))
                bn_chain(dve.tensor_tensor(b(6), b(0), b(5), ALU.mult))
                bn_chain(dve.tensor_tensor(b(7), cols[0:C, be:be + 1], b(6), ALU.subtract))

            edges(EC1)
            batch_norm(EC1, GA1, BE1)
            for t, j in ((a1, 5), (c1, 7)):
                bn_chain(dve.tensor_copy(t[0:C, :], bn[0:C, j:j + 1]))
                bn_chain(dve.tensor_copy(t[C:P, :], bn[0:C, j:j + 1]))
            bn_chain(dve.tensor_scalar(Weff[:, :], Wc[1][:, :], a1[:, :], None, ALU.mult))
            dve.wait_ge(s_bnp, 1)
            bn_chain(dve.tensor_tensor(bias2[:, :], pS[0][0:C, 8:9], cols[0:C, B2A:B2A + 1], ALU.add))
            bn_chain(dve.memset(acc[:, :, :], 0.0))
            dve.drain().then_inc(s_fold, 1)
            BN1_STEPS = bn_steps[0]
            edges(EC2)
            batch_norm(EC2, GA2, BE2)
            for j, c in ((0, 5), (1, 7)):
                bn_chain(dve.tensor_scalar(diag[:, j, :], ident[0:C, 0:C], bn[0:C, c:c + 1], None, ALU.mult))
            dve.wait_ge(s_bnp, 2)
            bn_chain(dve.tensor_copy(bnrow[:, :, :], pU1[:, 0:2 * C].rearrange("p (j c) -> p j c", j=2)))
            dve.drain().then_inc(s_fold, 1)

            def squares(h, s):
                dve.wait_ge(s_dsq, 2 * h + s + 1)
                dve.tensor_reduce(ln[s][:, 2, :], sq[s][:, :, :], AX, ALU.add).then_inc(s_ssq, 1)

            def factors(h, s):
                n = 2 * h + s + 1
                m = NG + n
                d = dis[:, bass.ds(2 * h + s, 1), :].rearrange("p a r -> p (a r)")
                dve.wait_ge(s_std, m)
                dve.reciprocal(ln[s][:, 4, :], ln[s][:, 3, :]).then_inc(s_rstd, 1)
                dve.wait_ge(s_rstd, m)
                dve.wait_ge(s_dis, n)
                need(dve, s_o, n - 2)
                dve.tensor_tensor(ln[s][:, 4, :], ln[s][:, 4, :], d, ALU.mult).then_inc(s_drs, 1)

            def stream(h, s, slot, rounds):
                n = 2 * h + s + 1
                m = NG + n
                first = isinstance(h, int) and h == 0 and s == 0
                prev = (h, 0) if s == 1 else (h - 1, 1)
                d = dis[:, bass.ds(2 * h + s, 1), :].rearrange("p a r -> p (a r)")
                dve.wait_ge(s_v, 2 * n)
                if not (isinstance(h, int) and h < 2):
                    dve.wait_ge(s_x1w[slot], 16 * (rounds - 1))
                dve.tensor_tensor(X1[slot][:, :, :], U[s][:, :, :], V[s][:, :, :], ALU.add).then_inc(s_x1, 1)
                if not first:
                    squares(*prev)
                dve.wait_ge(s_x1, n)
                dve.tensor_reduce(ln[s][:, 0, :], X1[slot][:, :, :], AX, ALU.add).then_inc(s_sum, 1)
                dve.wait_ge(s_sum, m)
                dve.tensor_scalar(ln[s][:, 1, :], ln[s][:, 0, :], 1.0 / C, None, ALU.mult).then_inc(s_mean, 1)
                dve.wait_ge(s_mean, m)
                need(dve, s_o, n - 4)
                dve.tensor_tensor(XC[slot], X1[slot][:, :, :], ln[s][:, 1, :].unsqueeze(2).to_broadcast([P, R, C]), ALU.subtract).then_inc(s_xc, 1)
                dve.wait_ge(s_deg, n)
                dve.reciprocal(d, deg[s][:, :]).then_inc(s_dis, 1)
                if not first:
                    factors(*prev)

            run_dense(dve, stream)
            squares(NG // 2 - 1, 1)
            factors(NG // 2 - 1, 1)

            def dis_rows(v, j):
                return dis[:, bass.ds(node_group(v, j), 1), :].rearrange("p a r -> p (a r)").unsqueeze(2).to_broadcast([P, R, C])

            def gcn_operands(v):
                n = lambda j: 2 * v + j + 1 + s_credit
                for j in range(2):
                    dve.wait_ge(s_ld[1][j], 32 * (v + 1))
                    dve.tensor_tensor(U[j][:, :, :], DA[j][:, :, :], DC[j][:, :, :], ALU.add).then_inc(s_used, 1)
                    dve.wait_ge(s_used, n(j))
                    dve.wait_ge(s_zT, n(j) - 2)
                    held(dve)
                    dve.tensor_tensor(Z[j][:, :, :], U[j][:, :, :], dis_rows(v, j), ALU.mult).then_inc(s_z, 1)

            def gcn_result(j):
                def part(v):
                    dve.wait_ge(s_gm, 2 * v + j + 1 + s_credit)
                    dve.wait_ge(s_wr[1][j], 16 * (v + 1))
                    held(dve)
                    dve.tensor_tensor(O[j][:, :, :], pG[:, :].rearrange("p (r c) -> p r c", c=C), dis_rows(v, j), ALU.mult).then_inc(s_o, 1)
                return part

            def final_operands(v):
                n = lambda j: 2 * v + j + 1
                for j in range(2):
                    dve.wait_ge(s_ld[2][j], 48 * (v + 1))
                    dve.tensor_tensor(U[j][:, :, :], DA[j][:, :, :], DC[j][:, :, :], ALU.add).then_inc(s_f0, 1)
                    dve.wait_ge(s_f0, n(j))
                    held(dve)
                    dve.tensor_tensor(Z[j][:, :, :], U[j][:, :, :], dis_rows(v, j), ALU.mult).then_inc(s_f1, 1)

            def final_results(v):
                n = lambda j: 2 * v + j + 1
                for j in range(2):
                    dve.wait_ge(s_f1, n(j))
                    dve.tensor_tensor(U[j][:, :, :], Z[j][:, :, :], gb2r[:, :].unsqueeze(1).to_broadcast([P, R, C]), ALU.add).then_inc(s_f2, 1)
                    dve.wait_ge(s_f2, n(j))
                    dve.wait_ge(s_wr[2][j], 16 * (v + 1))
                    dve.scalar_tensor_tensor(O[j][:, :, :], U[j][:, :, :], 0.0, V[j][:, :, :], ALU.max, ALU.add).then_inc(s_o, 1)

            def gcn_unit(v):
                for part in (gcn_operands, gcn_result(0), gcn_result(1)):
                    part(v)

            def final_unit(v):
                final_operands(v)
                final_results(v)

            dve.sem_inc(s_used, s_credit)
            dve.sem_inc(s_z, s_credit)
            edges(GCN1, (gcn_result(0),), (gcn_result(1),), (gcn_operands,))
            remaining(dve, gcn_unit)
            edges(GCN2, this_end=(final_unit,))
            remaining(dve, final_unit)

        @block.tensor
        def _(pe):
            pe.wait_ge(s_rows, 1)
            for a in range(8):
                for c in range(CH):
                    last = pe.transpose(bank[a][:, c * P:(c + 1) * P], rows[:, a, c, :], ident[:, :])
            last.then_inc(s_rowsT, 1)
            pe.wait_ge(s_idx, 8)
            for c in range(CH):
                last = pe.matmul(bank[0][:, c * P:(c + 1) * P], rows[:, 8, c, P - 1:P].to_broadcast([P, P]), ident[:, :], start=True, stop=True)
            last.then_inc(s_last, 1)
            pe.wait_ge(s_ready, 1)
            pe.matmul(bank[1][0:1, 0:NG], ones[0:UNITS, 0:1], ready[0:UNITS, :], start=True, stop=True).then_inc(s_avail, 1)
            pe.wait_ge(s_plan, 1)
            def edges(ph, first_half=(), second_half=()):
                conv = ph in (EC1, EC2)
                width = CB if ph == EC2 else C

                def spread_flags(h, s):
                    n = done(ph, h, s)
                    pe.wait_ge(s_fl, n)
                    need(pe, s_scan, n - 2 if conv else n - 1)
                    for k in range(K):
                        last = pe.matmul((pF[s] if conv else pFg)[:, k * P:(k + 1) * P], fl[s][:, k:k + 1].to_broadcast([P, P]), ident16[:, :], start=True, stop=True)
                    last.then_inc(s_flT, 1)

                def turn_rows(h, s):
                    n = done(ph, h, s)
                    need(pe, s_TS, n - 1)
                    if ph == EC1:
                        pe.wait_ge(s_h, n)
                        for k in range(K):
                            last = pe.transpose(pT[:, k * P:(k + 1) * P], H[s][:, k, :], ident[:, :])
                        last.then_inc(s_T, 1)
                    else:
                        pe.wait_ge(s_g[s], gath(ph, h))
                        held(pe)
                        for k in range(K):
                            last = pe.transpose(pT[0:C, k * P:(k + 1) * P], G[s][:, k, 0:C], ident[:, :])
                        last.then_inc(s_T, 1)

                def turn_result(h, s):
                    n = done(ph, h, s)
                    pe.wait_ge(s_scan, n)
                    need(pe, s_mt, n - 1)
                    if conv:
                        need(pe, s_mq, n - 1)
                    held(pe)
                    for k in range(K):
                        last = pe.transpose(pBk[:, k, 0:width], M[s][0:width, k * P:(k + 1) * P], ident[0:width, 0:width])
                    last.then_inc(s_mT, 1)

                def stats(h, s):
                    n = done(ph, h, s)
                    pe.wait_ge(s_mk, n)
                    pe.wait_ge(s_mq, n)
                    need(pe, s_acc, n - 2)
                    for k in range(K):
                        last = pe.matmul(pS[s][0:1, 0:2 * C], mk[s][:, k:k + 1], MT[s][:, k, :, 0:C], start=k == 0, stop=k == K - 1)
                    last.then_inc(s_st, 1)

                def layer1(h, s):
                    n = done(ph, h, s)
                    pe.wait_ge(s_TS, n)
                    if ph == EC2:
                        pe.wait_ge(s_back, n - NG)
                    need(pe, s_a1, n - 1)
                    pe.matmul(pU1[0:C, :], (Wc[0] if ph == EC1 else Weff)[:, :], TS[s][:, :], start=True, stop=True).then_inc(s_u1, 1)

                def layer2(h, s):
                    n = done(ph, h, s)
                    pe.wait_ge(s_a1, n)
                    need(pe, s_a2, n - 1)
                    held(pe)
                    pe.matmul(pU2[0:C, :], Wb[0 if ph == EC1 else 1][:, :], A1[:, :], start=True, stop=True).then_inc(s_u2, 1)

                def step(h, s):
                    first = isinstance(h, int) and h == 0 and s == 0
                    prev = (h, 0) if s == 1 else (h - 1, 1)
                    if conv:
                        spread_flags(h, s)
                        turn_rows(h, s)
                    else:
                        turn_rows(h, s)
                        spread_flags(h, s)
                    if conv and not first:
                        layer2(*prev)
                    if conv:
                        layer1(h, s)
                    if conv and not (isinstance(h, int) and h == 0):
                        stats(h - 1, s)
                    if not first:
                        turn_result(*prev)

                def gcn_pair(h):
                    step(h, 0)
                    this = plan_at(pe, h) if first_half else None
                    planned(pe, this, *first_half)
                    step(h, 1)
                    planned(pe, this, *second_half)

                if conv:
                    run(pe, step)
                else:
                    run_pairs(pe, gcn_pair)
                if conv:
                    layer2(NG // 2 - 1, 1)
                    stats(NG // 2 - 1, 0)
                turn_result(NG // 2 - 1, 1)
                if conv:
                    stats(NG // 2 - 1, 1)
                    pe.wait_ge(s_acc, NG * (ph + 1))
                    for j in range(2):
                        last = pe.matmul(pS[0][0:C, j:j + 1], acc[0:1, j, :], ones[0:1, 0:1], start=True, stop=True)
                    last.then_inc(s_bnc, 1)

            pe.wait_ge(s_wcat, 2)
            edges(EC1)
            pe.wait_ge(s_bn, 8 + 5)
            pe.matmul(pS[0][0:C, 8:9], Wc[1][:, :], c1[:, :], start=True, stop=True).then_inc(s_bnp, 1)
            pe.wait_ge(s_fold, 1)
            edges(EC2)
            pe.wait_ge(s_bn, 8 + 5 + 2 + 8 + 2)
            for j in range(2):
                last = pe.matmul(pU1[:, j * C:(j + 1) * C], ones[0:C, 0:P], diag[:, j, :], start=True, stop=True)
            last.then_inc(s_bnp, 1)

            count = lambda v, j: 2 * v + j + 1 + s_credit

            def turn_sums(v):
                for j in range(2):
                    pe.wait_ge(s_z, count(v, j))
                    pe.wait_ge(s_zTS, count(v, j) - 2)
                    for i in range(R // 2):
                        last = pe.transpose(pZT[j][:, i * P:(i + 1) * P], Z[j][:, 2 * i:2 * i + 2, :].rearrange("p r c -> p (r c)"), ident[:, :])
                    last.then_inc(s_zT, 1)

            def products(j):
                def part(v):
                    n = count(v, j)
                    pe.wait_ge(s_zTS, n)
                    for half in range(2):
                        pe.wait_ge(s_hr, 2 * (n - 1) - 1 + half)
                        pe.matmul(pH[half][:, :], gw1[half * C:(half + 1) * C, :], ZT[j][half * C:(half + 1) * C, :], start=True, stop=True).then_inc(s_hm, 1)
                    pe.wait_ge(s_o, ND + 2 * v + j)
                    for r in [*range(0, R, 2), *range(1, R, 2)]:
                        if r < 2:
                            pe.wait_ge(s_hr, 2 * n - 1 + r)
                        last = pe.matmul(pG[:, r * C:(r + 1) * C], HT[:, r % 2, (r // 2) * P:(r // 2 + 1) * P], gw2[:, :], start=True, stop=True)
                    last.then_inc(s_gm, 1)
                return part

            def gcn_unit(v):
                for part in (turn_sums, products(0), products(1)):
                    part(v)

            pe.sem_inc(s_zT, s_credit)
            pe.sem_inc(s_hm, 2 * s_credit)
            pe.sem_inc(s_gm, s_credit)
            edges(GCN1, (turn_sums, products(0)), (products(1),))
            remaining(pe, gcn_unit)
            edges(GCN2)


_INS = ["x", "src", "dst", "L0_gnn_W1a", "L0_gnn_b1a", "L0_gnn_W1b", "L0_gnn_b1b", "L0_gnn_gamma1", "L0_gnn_beta1",
        "L0_gnn_W2a", "L0_gnn_b2a", "L0_gnn_W2b", "L0_gnn_b2b", "L0_gnn_gamma2", "L0_gnn_beta2",
        "L1_gnn_W1", "L1_gnn_b1", "L1_gnn_W2", "L1_gnn_b2"]


def kernel(**inputs):
    import numpy as _np
    import concourse.bacc as _bacc
    from concourse import mybir as _mybir
    from concourse.bass_utils import run_bass_kernel_spmd as _run

    nc = _bacc.Bacc("TRN2", target_bir_lowering=False, num_devices=1)
    arrays, args = {}, []
    for name in _INS:
        a = _np.ascontiguousarray(inputs[name])
        arrays[f"in_{name}"] = a
        args.append(nc.dram_tensor(f"in_{name}", a.shape, _mybir.dt.from_np(a.dtype), kind="ExternalInput").ap())
    args.append(nc.dram_tensor("out_0", (N, C), F32, kind="ExternalOutput").ap())
    build(nc, *args)
    r = _run(nc, [arrays], core_ids=[0])
    return r.results[0]["out_0"]
```
